# Optimizing a Trainium2 kernel written in Bass

```python
import numpy as np
import jax
import jax.numpy as jnp

def _softmax(x, axis=-1):
    return jax.nn.softmax(x, axis=axis)
def _gelu(x):
    return jax.nn.gelu(x, approximate=True)
def _silu(x):
    return jax.nn.silu(x)
def _sigmoid(x):
    return jax.nn.sigmoid(x)
def _layernorm(x, axis=-1, eps=1e-5):
    m = jnp.mean(x, axis=axis, keepdims=True)
    v = jnp.var(x, axis=axis, keepdims=True)
    return (x - m) / jnp.sqrt(v + eps)
def _scatter_add(tgt, idx, src, axis=0):
    return tgt.at[idx].add(src)
def _segment_sum(src, seg, n):
    return jax.ops.segment_sum(src, seg, n)

kernel_name = 'mk_adj_ffn_d1_adj_512_6ccd2b'

def setup_inputs(seed: int = 0):
    np.random.seed(seed)
    _w = jnp.asarray
    def _rec_inputs():
        import jax
        import jax.numpy as jnp
        _gk = jax.random.key(seed)
        x = -0.0002928 + 1 * jax.random.normal(jax.random.fold_in(_gk, 1), (3327, 512), jnp.float32)
        _a = jax.random.bernoulli(jax.random.fold_in(_gk, 2), 0.00480914, (3327, 3327))
        _a = jnp.logical_or(_a, jnp.swapaxes(_a, -1, -2))
        _a = jnp.logical_or(_a, jnp.eye(3327, dtype=bool))
        _af = _a.astype(jnp.float32)
        _af = _af * jax.random.uniform(jax.random.fold_in(_gk, 3), (3327, 3327), jnp.float32, 0.05, 1)
        adj = _af
        return x, adj
    x, adj = _rec_inputs()
    def _L0_gnn_setup():
        import jax, jax.numpy as jnp
        import numpy as np
        N = 8192
        IN_C = 512
        OUT_C = 512
        key = jax.random.key(seed)
        k1, k2, k3 = jax.random.split(key, 3)
        x = jax.random.normal(k1, (N, IN_C), dtype=jnp.float32)
        adj = jax.random.uniform(k2, (N, N), dtype=jnp.float32)
        w = jax.random.uniform(k3, (IN_C, OUT_C), dtype=jnp.float32)
        return {'x': x, 'adj': adj, 'w': w}
    _L0_gnn_all = _L0_gnn_setup()
    _L0_gnn_in = {k: v for k, v in _L0_gnn_all.items() if k in ('w', )}
    del _L0_gnn_all

    def _L0_ffn_setup():
        import jax, jax.numpy as jnp
        import numpy as np
        E = 8
        TOP_K = 2
        D = 512
        H = 1024
        B, S = (16, 4096)
        key = jax.random.key(seed)
        ks = jax.random.split(key, 10)
        sd = lambda fan_in: 1.0 / np.sqrt(fan_in)
        x = jax.random.normal(ks[0], (B, S, D), dtype=jnp.float32)
        gw1 = jax.random.uniform(ks[1], (D, D // 2), jnp.float32, -sd(D), sd(D))
        gb1 = jnp.zeros((D // 2,), jnp.float32)
        gw2 = jax.random.uniform(ks[2], (D // 2, E), jnp.float32, -sd(D // 2), sd(D // 2))
        gb2 = jnp.zeros((E,), jnp.float32)
        we1 = jax.random.uniform(ks[3], (E, D, H), jnp.float32, -sd(D), sd(D))
        be1 = jnp.zeros((E, H), jnp.float32)
        we2 = jax.random.uniform(ks[4], (E, H, D), jnp.float32, -sd(H), sd(H))
        be2 = jnp.zeros((E, D), jnp.float32)
        return {'x': x, 'gw1': gw1, 'gb1': gb1, 'gw2': gw2, 'gb2': gb2, 'we1': we1, 'be1': be1, 'we2': we2, 'be2': be2}
    _L0_ffn_all = _L0_ffn_setup()
    _L0_ffn_in = {k: v for k, v in _L0_ffn_all.items() if k in ('gw1', 'gb1', 'gw2', 'gb2', 'we1', 'be1', 'we2', 'be2', )}
    del _L0_ffn_all

    return {
        "x": x,
        "adj": adj,
        "L0_gnn_w": _L0_gnn_in["w"],
        "L0_ffn_gw1": _L0_ffn_in["gw1"],
        "L0_ffn_gb1": _L0_ffn_in["gb1"],
        "L0_ffn_gw2": _L0_ffn_in["gw2"],
        "L0_ffn_gb2": _L0_ffn_in["gb2"],
        "L0_ffn_we1": _L0_ffn_in["we1"],
        "L0_ffn_be1": _L0_ffn_in["be1"],
        "L0_ffn_we2": _L0_ffn_in["we2"],
        "L0_ffn_be2": _L0_ffn_in["be2"],
    }

def reference(x, adj, L0_gnn_w, L0_ffn_gw1, L0_ffn_gb1, L0_ffn_gw2, L0_ffn_gb2, L0_ffn_we1, L0_ffn_be1, L0_ffn_we2, L0_ffn_be2):
    import jax
    import jax.numpy as jnp
    def _L0_gnn_ref(x, adj, w):
        import jax, jax.numpy as jnp
        import numpy as np
        N = 8192
        IN_C = 512
        OUT_C = 512
        A = adj + jnp.eye(adj.shape[0], dtype=adj.dtype)
        deg = jnp.sum(A, axis=1)
        d_inv_sqrt = jax.lax.rsqrt(deg)
        A_hat = A * d_inv_sqrt[:, None] * d_inv_sqrt[None, :]
        mm_1 = A_hat @ x
        return jax.nn.elu(mm_1 @ w)

    def _L0_ffn_ref(x, gw1, gb1, gw2, gb2, we1, be1, we2, be2):
        import jax, jax.numpy as jnp
        import numpy as np
        E = 8
        TOP_K = 2
        D = 512
        H = 1024
        B, S = (16, 4096)
        b, s, d = x.shape
        xf = x.reshape(-1, d)
        T = xf.shape[0]
        gate_logits = jax.nn.relu(xf @ gw1 + gb1) @ gw2 + gb2
        gate_weights = jax.nn.softmax(gate_logits, axis=-1)
        top_w, top_idx = jax.lax.top_k(gate_weights, TOP_K)
        top_w = jax.nn.softmax(top_w, axis=-1)
        combine = jnp.zeros((T, E), dtype=xf.dtype)
        combine = combine.at[jnp.arange(T)[:, None], top_idx].add(top_w)
        out = jnp.zeros_like(xf)
        for e in range(E):
            h = jax.nn.gelu(xf @ we1[e] + be1[e], approximate=False)
            y = h @ we2[e] + be2[e]
            out = out + combine[:, e:e + 1] * y
        return out.reshape(b, s, d)

    x = x + _L0_gnn_ref(_layernorm(x, axis=-1), adj, L0_gnn_w)
    x = x + _L0_ffn_ref((_layernorm(x, axis=-1))[None], L0_ffn_gw1, L0_ffn_gb1, L0_ffn_gw2, L0_ffn_gb2, L0_ffn_we1, L0_ffn_be1, L0_ffn_we2, L0_ffn_be2)[0]
    return x


_drawn_inputs = setup_inputs


def setup_inputs(seed=0):
    import zlib

    import numpy as np

    out = dict(_drawn_inputs(seed))
    spreads = {'L0_ffn_gb1': (0.0, 0.1),
     'L0_ffn_gb2': (0.0, 0.1),
     'L0_ffn_be1': (0.0, 0.468),
     'L0_ffn_be2': (0.0, 0.1)}
    factors = {}
    for name, (base, spread) in spreads.items():
        noise = np.random.default_rng([zlib.crc32(name.encode()), seed]).standard_normal(out[name].shape)
        drawn = base * np.exp(spread * noise) if base else spread * noise
        out[name] = jnp.asarray(drawn.astype(out[name].dtype))
    for name, factor in factors.items():
        out[name] = (out[name] * factor).astype(out[name].dtype)
    return out
```

```python
import concourse.bass as bass
from concourse import mybir
from contextlib import ExitStack

F32 = mybir.dt.float32
F32R = mybir.dt.float32r
BF16 = mybir.dt.bfloat16
I32 = mybir.dt.int32
U32 = mybir.dt.uint32
ALU = mybir.AluOpType
ACT = mybir.ActivationFunctionType
AX = mybir.AxisListType

P = 128
N_TOK = 3327
NT = -(-N_TOK // P)
NP = NT * P
D = 512
DC = D // P
GH = 256
GC = GH // P
E = 8
H = 1024
HC = H // P
TOP_K = 2
EPS = 1e-5

S_ROWS = 256
SJ = S_ROWS // P
CAP = -(-NP // S_ROWS) * S_ROWS
STEPS = (TOP_K * NP + E * (S_ROWS - 1)) // S_ROWS
DUMMY = NP
ROWS = NP + S_ROWS
SLOTS = (E + 1) * CAP

CW = 512
CT = CW // P
NCH = -(-NP // CW)
RING = 4


def build(nc, x, adj, adj_t, w, gw1, gb1, gw2, gb2, we1, be1, we2, be2, out):
    ctx = ExitStack()
    with ctx:
        arena = [-(-nc.sbuf_base // 32) * 32]

        def at(name, shape, dt):
            n = 1
            for k in shape[1:]:
                n *= k
            size = -(-n * (2 if dt == BF16 else 4) // 32) * 32
            t = nc.alloc_sbuf_tensor_at(name, shape, dt, offset=arena[0])
            arena[0] += size
            return t

        def sem(name):
            return ctx.enter_context(nc.semaphore(name))

        ident = at("ident", [P, P], F32)
        ones = at("ones", [P, P], F32)
        upper = at("upper", [P, P], BF16)
        ones_bf = at("ones_bf", [P, P], BF16)
        ln_add = at("ln_add", [P, 2], F32)
        ln_pow = at("ln_pow", [P, 2], F32)
        sched = at("sched", [P, STEPS, 2], I32)
        cols8 = at("cols8", [P, E], F32)
        tok_id = at("tok_id", [P, NT], I32)
        base0 = at("base0", [P, E], F32)
        base = at("base", [P, E], F32)
        common_end = arena[0]

        xs_hi = at("xs_hi", [P, NT, D], F32R)
        xs_lo = at("xs_lo", [P, NT, D], F32R)
        xs_end = arena[0]
        a_raw = at("a_raw", [P, RING, CW], F32)
        a_hi = at("a_hi", [P, RING, CW], F32R)
        a_lo = at("a_lo", [P, RING, CW], F32R)
        m_at = arena[0]
        m_raw = at("m_raw", [P, 2, CT, D], F32)
        mt_at = arena[0]
        mt_hi = at("mt_hi", [P, 2, DC, P], F32R)
        mt_lo = at("mt_lo", [P, 2, DC, P], F32R)
        x_in = at("x_in", [P, 2, D], F32)
        x_n = at("x_n", [P, 2, D], F32)
        e_at = arena[0]
        e_buf = at("e_buf", [P, 2, D], F32)
        stat6 = at("stat6", [P, 2, 6], F32)
        mv = at("mv", [P, NT, 2], F32)
        pk = at("pk", [P, 2, 2], F32)
        rs = at("rs", [P, NT, 2], F32)
        scl = at("scl", [P, NT], F32)
        deg = at("deg", [P, NT], F32)
        gb1_sb = at("gb1_sb", [P, GC], F32)
        gw2_sb = at("gw2_sb", [P, GC, E], F32)
        gb2_sb = at("gb2_sb", [P, E], F32)
        mv2 = at("mv2", [P, 2, 2], F32)
        pk2 = at("pk2", [P, 2, 1], F32)
        rstd2 = at("rstd2", [P, 2, 1], F32)
        lg = at("lg", [P, 2, E], F32)
        lmax = at("lmax", [P, 2], F32)
        lc = at("lc", [P, 2, E], F32)
        le = at("le", [P, 2, E], F32)
        lsum = at("lsum", [P, 2], F32)
        lrec = at("lrec", [P, 2], F32)
        prob = at("prob", [P, 2, E], F32)
        top = at("top", [P, 2, 8], F32)
        topi = at("topi", [P, 2, 8], U32)
        topf = at("topf", [P, 2, 8], F32)
        hot = at("hot", [P, 2, TOP_K, E], F32)
        mask = at("mask", [P, 2, E], BF16)
        pd = at("pd", [P, 2], F32)
        pe2 = at("pe2", [P, 2], F32)
        pden = at("pden", [P, 2], F32)
        wts = at("wts", [P, 2, TOP_K], F32)
        rb = at("rb", [P, 2, E], F32)
        pick = at("pick", [P, 2, TOP_K, E], F32)
        slotf = at("slotf", [P, 2, TOP_K], F32)
        slot = at("slot", [P, 2, 2, TOP_K], I32)
        pay = at("pay", [P, 2, 2, TOP_K, 2], I32)
        cnt = at("cnt", [P, E], F32)
        tiles_i = at("tiles_i", [P, E], I32)
        tiles_f = at("tiles_f", [P, E], F32)
        cum = at("cum", [P, 4, E], F32)
        s_i = at("s_i", [P, STEPS], F32)
        past = at("past", [P, STEPS, E], F32)
        past_t = at("past_t", [P, STEPS, E], F32)
        s_e = at("s_e", [P, STEPS], F32)
        s_t = at("s_t", [P, STEPS], F32)
        s_r = at("s_r", [P, STEPS, 2], F32)
        rows_at = arena[0]
        row_in = at("row_in", [P, 2, NP], F32)
        rows_end = arena[0]
        arena[0] = rows_at
        w_hi = at("w_hi", [P, DC, D], F32R)
        w_lo = at("w_lo", [P, DC, D], F32R)
        gw1_hi = at("gw1_hi", [P, DC, GH], F32R)
        xt_hi = at("xt_hi", [P, DC, 2 * P], F32R)
        g_t = at("g_t", [P, GC, 2 * P], F32)
        arena[0] = max(arena[0], rows_end)
        gw1_lo = at("gw1_lo", [P, DC, GH], F32R)
        xt_lo = at("xt_lo", [P, DC, 2 * P], F32R)

        def over(name, shape, dt, place):
            return nc.alloc_sbuf_tensor_at(name, shape, dt, offset=place)

        w_raw = over("w_raw", [P, DC, D], F32, mt_at)
        gw1_raw = over("gw1_raw", [P, DC, GH], F32, e_at)
        PRE = SLOTS // P
        pre = over("pre", [P, PRE, 2], I32, m_at)
        zrow = over("zrow", [P, SJ, D], F32, m_at + CT * D * 4)

        arena[0] = common_end
        w1_raw = at("w1_raw", [P, DC, H], F32)
        w2_raw = at("w2_raw", [P, HC, D], F32)
        w1_hi = at("w1_hi", [P, DC, H], F32R)
        w1_lo = at("w1_lo", [P, DC, H], F32R)
        w2_hi = at("w2_hi", [P, HC, D], F32R)
        w2_lo = at("w2_lo", [P, HC, D], F32R)
        x_g = at("x_g", [P, SJ, D], F32)
        xe_hi = at("xe_hi", [P, DC, S_ROWS], F32R)
        xe_lo = at("xe_lo", [P, DC, S_ROWS], F32R)
        h_hi = at("h_hi", [P, HC, S_ROWS], F32R)
        h_lo = at("h_lo", [P, HC, S_ROWS], F32R)
        y_sb = at("y_sb", [P, SJ, D], F32)
        be1_sb = at("be1_sb", [P, HC], F32)
        be2_sb = at("be2_sb", [P, D], F32)
        list_g = at("list_g", [P, SJ, 2], I32)
        list_y = at("list_y", [P, SJ, 2], I32)

        bank = [ctx.enter_context(nc.psum_tensor(f"bank{b}", [P, 512], F32)) for b in range(8)]
        BY, BG, BS = 4, 6, 7
        L_AT, R_AT, C_AT = 0, 32, 64

        xln = nc.dram_tensor("xln", (ROWS, D), F32).ap()
        lists = nc.dram_tensor("lists", (SLOTS, 2), I32).ap()

        consts = sem("consts")
        const_ld = sem("const_ld")
        w_ld = sem("w_ld")
        a_ld = [sem(f"a_ld{i}") for i in range(RING)]
        x_ld = [sem(f"x_ld{i}") for i in range(2)]
        row_ld = [sem(f"row_ld{i}") for i in range(2)]
        pre_st = sem("pre_st")
        pre_rdy = sem("pre_rdy")
        deg_done = sem("deg_done")
        mv_done = sem("mv_done")
        scl_done = sem("scl_done")
        xn_done = sem("xn_done")
        xs_hi_done = sem("xs_hi_done")
        xs_lo_done = sem("xs_lo_done")
        a_hi_done = sem("a_hi_done")
        a_lo_done = sem("a_lo_done")
        unit_done = sem("unit_done")
        m_ready = sem("m_ready")
        m_evac = sem("m_evac")
        m_full = sem("m_full")
        w_hi_done = sem("w_hi_done")
        w_lo_done = sem("w_lo_done")
        mt_ready = sem("mt_ready")
        mt_hi_done = sem("mt_hi_done")
        mt_lo_done = sem("mt_lo_done")
        y_ready = sem("y_ready")
        neg_done = sem("neg_done")
        exp_done = sem("exp_done")
        x1_done = sem("x1_done")
        mv2_done = sem("mv2_done")
        rstd2_done = sem("rstd2_done")
        xl_done = sem("xl_done")
        x1_st = [sem(f"x1_st{i}") for i in range(2)]
        xln_st = [sem(f"xln_st{i}") for i in range(2)]
        xt_ready = sem("xt_ready")
        xt_hi_done = sem("xt_hi_done")
        xt_lo_done = sem("xt_lo_done")
        g_ready = sem("g_ready")
        g_done = sem("g_done")
        l_ready = sem("l_ready")
        lc_done = sem("lc_done")
        le_done = sem("le_done")
        pd_done = sem("pd_done")
        pe2_done = sem("pe2_done")
        mask_done = sem("mask_done")
        r_ready = sem("r_ready")
        route_done = sem("route_done")
        list_st = sem("list_st")
        sched_done = sem("sched_done")
        dve_own = sem("dve_own")
        pool_own = sem("pool_own")
        phase1 = sem("phase1")
        lg_ld = sem("lg_ld")
        ly_ld = sem("ly_ld")
        w1_ld = [sem(f"w1_ld{i}") for i in range(4)]
        w2_ld = [sem(f"w2_ld{i}") for i in range(4)]
        be1_ld = sem("be1_ld")
        be2_ld = sem("be2_ld")
        xg_ld = sem("xg_ld")
        xe_ready = sem("xe_ready")
        xe_hi_done = sem("xe_hi_done")
        xe_lo_done = sem("xe_lo_done")
        w1_hi_done = sem("w1_hi_done")
        w1_lo_done = sem("w1_lo_done")
        w2_hi_done = sem("w2_hi_done")
        w2_lo_done = sem("w2_lo_done")
        h_ready = sem("h_ready")
        gelu_done = sem("gelu_done")
        h_hi_done = sem("h_hi_done")
        h_lo_done = sem("h_lo_done")
        w2_used = sem("w2_used")
        ye_ready = sem("ye_ready")
        yb_done = sem("yb_done")
        yw_done = sem("yw_done")
        y_add = sem("y_add")
        waited = sem("waited")

        units = [(0, j, c) for j in range(NT) for c in range(2)]
        for g in range(1, NCH - 1):
            units += [(g, j, g + 1) for j in range(NT)]
        NU = len(units)
        first_unit = {}
        for u, (g, j, c) in enumerate(units):
            first_unit.setdefault(g, u)
        NG = NCH - 1
        N_PAIR = NT // 2

        def chunk_tiles(c):
            return min(CT, NT - c * CT)

        pair_at, todo = {}, {1: [0, 1, 2, 3]}
        for g in range(2, NG):
            todo[g] = [2 * g, 2 * g + 1]
        for g, pairs in todo.items():
            for n, p in enumerate(pairs):
                pair_at[p] = first_unit[g] + 1 + n * (5 if g == 1 else 12)
        LAST = N_PAIR - 1
        pair_at[LAST] = NU + 8
        STAGE = {"mt": 1, "y0": 2, "y1": 3, "xt": 5, "gate": 6, "logit": 7, "rank": 8}
        REACT = RING

        def events(stages, shift):
            found = {}
            for p in range(N_PAIR):
                for name, fn in stages:
                    found.setdefault(pair_at[p] + STAGE[name] + shift, []).append((fn, p))
            return found

        def run(found, u):
            for fn, p in found.pop(u, ()):
                fn(p)

        def finish(found):
            for u in sorted(found):
                run(found, u)

        def bank_of(g, c, i):
            return bank[(c * CT if g == 0 else 0) + i]

        def dinv(t):
            return rs[:, t, 1:2]

        def wait_unit(eng, u):
            if units[u][1] == NT - 1:
                eng.wait_ge(m_ready, min((units[u][2] + 1) * CT, NT))
            else:
                eng.wait_ge(unit_done, sum(1 for v in units[:u + 1] if v[1] < NT - 1))

        block = ctx.enter_context(nc.Block())

        @block.sync
        def _(sp):
            def load_x(t, q, n):
                sp.dma_start(x_in[:, q, :], x[t * P:(t + 1) * P, :]).then_inc(x_ld[q], 16)

            def load_pair_x(p):
                for q in range(2):
                    if p == 0:
                        sp.wait_ge(xn_done, NT - 1 + q)
                    else:
                        sp.wait_ge(x1_st[q], 16 * p)
                        sp.wait_ge(xl_done, 2 * p - 1 + q)
                    load_x(2 * p + q, q, p)

            post = events([("y0", load_pair_x)], 2)
            for u, (g, j, c) in enumerate(units):
                run(post, u)
                if g == 0 and c == 0:
                    if j >= 2:
                        sp.wait_ge(xn_done, j - 1)
                    load_x(j, j % 2, j)
                    if j >= 2:
                        sp.wait_ge(deg_done, j - 1)
                    sp.dma_start(row_in[:, j % 2, :], adj[j * P:(j + 1) * P, :]).then_inc(row_ld[j % 2], 16)
                if u >= RING:
                    sp.wait_ge(a_lo_done, u - RING + 1)
                n = chunk_tiles(c) * P
                sp.dma_start(a_raw[:, u % RING, 0:n],
                             adj_t[j * P:(j + 1) * P, c * CW:c * CW + n]).then_inc(a_ld[u % RING], 16)
                if u == 3:
                    sp.dma_start(w_raw[:, :, :], w.rearrange("(c p) n -> p c n", p=P)).then_inc(w_ld, 16)
                    sp.dma_start(gw1_raw[:, :, :], gw1.rearrange("(c p) n -> p c n", p=P)).then_inc(w_ld, 16)
                    sp.dma_start(gw2_sb[:, :, :], gw2.rearrange("(c p) n -> p c n", p=P)).then_inc(const_ld, 16)
                    sp.dma_start(gb1_sb[:, :], gb1).then_inc(const_ld, 16)
                    sp.dma_start(gb2_sb[:, :], gb2.partition_broadcast(P)).then_inc(const_ld, 16)
            finish(post)
            sp.wait_ge(phase1, 2)

            def step_loads(s, first):
                row = sp.value_load(sched[0:1, s, 0:1], min_val=0, max_val=SLOTS - S_ROWS)
                ex = sp.value_load(sched[0:1, s, 1:2], min_val=0, max_val=E - 1)
                if not first:
                    sp.wait_ge(xg_ld, 32 * s)
                sp.dma_start(list_g[:, :, :], lists[bass.ds(row, S_ROWS), :]
                             .rearrange("(p j) c -> p j c", p=P)).then_inc(lg_ld, 16)
                for m in range(4):
                    if not first:
                        sp.wait_ge(w1_lo_done, 4 * (s - 1) + m + 1)
                    sp.dma_start(w1_raw[:, :, m * 256:(m + 1) * 256],
                                 we1[bass.ds(ex, 1), :, m * 256:(m + 1) * 256]
                                 .rearrange("o (c p) n -> p (o c) n", p=P)).then_inc(w1_ld[m], 16)
                if not first:
                    sp.wait_ge(gelu_done, HC * s)
                sp.dma_start(be1_sb[:, :], be1[bass.ds(ex, 1), :, :]
                             .rearrange("o p n -> (o p) n")).then_inc(be1_ld, 16)
                for m in range(4):
                    if not first:
                        sp.wait_ge(w2_lo_done, 4 * (s - 1) + m + 1)
                    sp.dma_start(w2_raw[:, 2 * m:2 * m + 2, :],
                                 we2[bass.ds(ex, 1), m * 256:(m + 1) * 256, :]
                                 .rearrange("o (c p) n -> p (o c) n", p=P)).then_inc(w2_ld[m], 16)

            step_loads(0, True)
            with sp.Fori(1, STEPS) as s:
                step_loads(s, False)

        @block.gpsimd
        def _(pool):
            own = [0]

            def link(ins):
                own[0] += 1
                ins.then_inc(pool_own, 1)
                pool.wait_ge(pool_own, own[0])

            pool.memset(ident[:, :], 0.0).then_inc(pool_own, 1)
            pool.memset(ones[:, :], 1.0).then_inc(pool_own, 1)
            pool.memset(ones_bf[:, :], 1.0).then_inc(pool_own, 1)
            pool.memset(ln_add[:, 0:1], EPS).then_inc(pool_own, 1)
            pool.memset(ln_add[:, 1:2], 1.0).then_inc(pool_own, 1)
            pool.memset(ln_pow[:, :], -0.5).then_inc(pool_own, 1)
            pool.memset(zrow[:, :, :], 0.0).then_inc(pool_own, 1)
            own[0] = 7
            pool.wait_ge(pool_own, own[0])
            link(pool.affine_select(out=ident[:, :], in_=ident[:, :], compare_op=ALU.not_equal, fill=1.0,
                                    base=0, pattern=[[-1, P]], channel_multiplier=1))
            link(pool.affine_select(out=upper[:, :], in_=ones_bf[:, :], compare_op=ALU.is_gt, fill=0.0,
                                    base=0, pattern=[[1, P]], channel_multiplier=-1))
            link(pool.iota(cols8[:, :], [[1, E]], base=0, channel_multiplier=0,
                           allow_small_or_imprecise_dtypes=True))
            link(pool.iota(base0[:, :], [[CAP, E]], base=0, channel_multiplier=0,
                           allow_small_or_imprecise_dtypes=True))
            link(pool.iota(s_i[:, :], [[1, STEPS]], base=0, channel_multiplier=0,
                           allow_small_or_imprecise_dtypes=True))
            link(pool.iota(tok_id[:, :], [[P, NT]], base=0, channel_multiplier=1))
            link(pool.iota(pre[:, :, 0], [[1, PRE]], base=0, channel_multiplier=PRE))
            pool.nop().then_inc(consts, 1)
            pool.dma_start(xln[NP:ROWS, :].rearrange("(j p) n -> p j n", p=P), zrow[:, :, :]).then_inc(pre_st, 16)
            pool.dma_start(out[NP:ROWS, :].rearrange("(j p) n -> p j n", p=P), zrow[:, :, :]).then_inc(pre_st, 16)
            pool.wait_ge(pre_rdy, 1)
            pool.dma_start(lists.rearrange("(p c) k -> p c k", p=P), pre[:, :, :]).then_inc(pre_st, 16)

            def norm_scale(j):
                k = j % 2
                pool.wait_ge(mv_done, j + 1)
                pool.wait_ge(deg_done, j + 1)
                link(pool.tensor_tensor(pk[:, k, 0:1], mv[:, j, 1:2], ln_add[:, 0:1], ALU.add))
                link(pool.tensor_tensor(pk[:, k, 1:2], deg[:, j:j + 1], ln_add[:, 1:2], ALU.add))
                link(pool.tensor_tensor(rs[:, j, :], pk[:, k, :], ln_pow[:, :], ALU.pow))
                pool.tensor_tensor(scl[:, j:j + 1], rs[:, j, 0:1], rs[:, j, 1:2], ALU.mult).then_inc(scl_done, 1)

            def add_self(c):
                for i in range(chunk_tiles(c)):
                    t = c * CT + i
                    pool.wait_ge(m_evac, t + 1)
                    pool.tensor_tensor(m_raw[:, c % 2, i, :], m_raw[:, c % 2, i, :],
                                       xs_lo[:, t, :].bitcast(F32), ALU.add).then_inc(m_full, 1)

            def norm2(p):
                for q in range(2):
                    t = 2 * p + q
                    pool.wait_ge(mv2_done, t + 1)
                    link(pool.tensor_tensor(pk2[:, q, :], mv2[:, q, 1:2], ln_add[:, 0:1], ALU.add))
                    pool.tensor_tensor(rstd2[:, q, :], pk2[:, q, :], ln_pow[:, 0:1], ALU.pow).then_inc(rstd2_done, 1)
                    pool.dma_start(out[t * P:(t + 1) * P, :], x_in[:, q, :]).then_inc(x1_st[q], 16)

            def store_rows(p):
                for q in range(2):
                    t = 2 * p + q
                    pool.wait_ge(xl_done, t + 1)
                    pool.dma_start(xln[t * P:(t + 1) * P, :], x_n[:, q, :]).then_inc(xln_st[q], 16)

            def scatter_lists(p):
                pool.wait_ge(route_done, p + 1)
                if p == 0:
                    pool.wait_ge(pre_st, 48)
                for q in range(2):
                    for k in range(TOP_K):
                        pool.indirect_dma_start(
                            out=lists[:, :], out_offset=bass.IndirectOffsetOnAxis(
                                ap=slot[:, p % 2, q, k:k + 1].bitcast(U32), axis=0),
                            in_=pay[:, p % 2, q, k, :], in_offset=None).then_inc(list_st, 16)

            for j in range(NT):
                norm_scale(j)
            work = []
            for c in range(NCH):
                g = max(c - 1, 0)
                work.append((first_unit.get(g + 1, NU), 0, add_self, c))
            for p in range(N_PAIR):
                work.append((pair_at[p] + STAGE["y1"], 1, norm2, p))
                work.append((pair_at[p] + STAGE["xt"], 2, store_rows, p))
                work.append((pair_at[p] + STAGE["rank"], 3, scatter_lists, p))
            for _, _, fn, n in sorted(work, key=lambda v: v[:2]):
                fn(n)
            pool.wait_ge(list_st, 16 * 2 * TOP_K * N_PAIR)
            for q in range(2):
                pool.wait_ge(x1_st[q], 16 * N_PAIR)
                pool.wait_ge(xln_st[q], 16 * N_PAIR)
            pool.nop().then_inc(phase1, 1)
            pool.wait_ge(phase1, 2)

            def load_for_y(s):
                row = pool.value_load(sched[0:1, s, 0:1], min_val=0, max_val=SLOTS - S_ROWS)
                ex = pool.value_load(sched[0:1, s, 1:2], min_val=0, max_val=E - 1)
                pool.dma_start(list_y[:, :, :], lists[bass.ds(row, S_ROWS), :]
                               .rearrange("(p j) c -> p j c", p=P)).then_inc(ly_ld, 16)
                pool.dma_start(be2_sb[:, :], be2[bass.ds(ex, 1), :]
                               .rearrange("o n -> (o n)").partition_broadcast(P)).then_inc(be2_ld, 16)

            def gather(s, first):
                pool.wait_ge(lg_ld, 16 * s + 16)
                if not first:
                    pool.wait_ge(xe_ready, SJ * s)
                pool.sem_inc(waited, 1)
                for jj in range(SJ):
                    pool.indirect_dma_start(
                        out=x_g[:, jj, :], out_offset=None, in_=xln[:, :],
                        in_offset=bass.IndirectOffsetOnAxis(
                            ap=list_g[:, jj, 0:1].bitcast(U32), axis=0)).then_inc(xg_ld, 16)

            def add_rows(s):
                for jj in range(SJ):
                    pool.wait_ge(yw_done, SJ * s + jj + 1)
                    pool.sem_inc(waited, 1)
                    pool.indirect_dma_start(
                        out=out[:, :], out_offset=bass.IndirectOffsetOnAxis(
                            ap=list_y[:, jj, 0:1].bitcast(U32), axis=0),
                        in_=y_sb[:, jj, :], in_offset=None, compute_op=ALU.add).then_inc(y_add, 16)
                    pool.wait_ge(y_add, 16 * (SJ * s + jj + 1))

            gather(0, True)
            load_for_y(0)
            gather(1, False)
            with pool.Fori(1, STEPS - 1) as s:
                gather(s + 1, False)
                add_rows(s - 1)
                load_for_y(s)
            add_rows(STEPS - 2)
            load_for_y(STEPS - 1)
            add_rows(STEPS - 1)

        @block.scalar
        def _(act):
            def evac_mt(p):
                for q in range(2):
                    act.wait_ge(mt_ready, 2 * p + q + 1)
                    act.activation(mt_hi[:, q, :, :], bank[BY + q][:, :].rearrange("p (c n) -> p c n", c=DC),
                                   ACT.Copy).then_inc(mt_hi_done, 1)

            def exp_neg(p, q):
                act.wait_ge(neg_done, 2 * p + q + 1)
                act.activation(e_buf[:, q, :], e_buf[:, q, :], ACT.Exp).then_inc(exp_done, 1)

            def evac_xt(p):
                for q in range(2):
                    act.wait_ge(xt_ready, 2 * p + q + 1)
                    act.activation(xt_hi[:, :, q * P:(q + 1) * P],
                                   bank[BY + q][:, :].rearrange("p (c n) -> p c n", c=DC),
                                   ACT.Copy).then_inc(xt_hi_done, 1)

            def relu_gate(p):
                act.wait_ge(g_ready, p + 1)
                for hb in range(GC):
                    act.activation(g_t[:, hb, :], bank[BG][:, hb * 256:(hb + 1) * 256], ACT.Relu,
                                   bias=gb1_sb[:, hb:hb + 1]).then_inc(g_done, 1)

            def exp_logits(p):
                act.wait_ge(lc_done, p + 1)
                act.activation(le[:, :, :], lc[:, :, :], ACT.Exp).then_inc(le_done, 1)
                act.wait_ge(pd_done, p + 1)
                act.activation(pe2[:, :], pd[:, :], ACT.Exp).then_inc(pe2_done, 1)

            post = events([("mt", evac_mt), ("y0", lambda p: exp_neg(p, 0)), ("y1", lambda p: exp_neg(p, 1)),
                           ("xt", evac_xt), ("gate", relu_gate), ("logit", exp_logits)], REACT)
            act.wait_ge(const_ld, 48)

            def degree(j):
                act.wait_ge(row_ld[j % 2], 16 * (j // 2 + 1))
                act.activation(row_in[:, j % 2, :], row_in[:, j % 2, :], ACT.Copy,
                               accum_out=deg[:, j:j + 1]).then_inc(deg_done, 1)

            def xs_split(j):
                act.wait_ge(xn_done, j + 1)
                act.activation(xs_hi[:, j, :], x_n[:, j % 2, :], ACT.Copy).then_inc(xs_hi_done, 1)

            degree(0)
            for u, (g, j, c) in enumerate(units):
                run(post, u)
                if g == 0 and c == 0:
                    if j + 1 < NT:
                        degree(j + 1)
                    xs_split(j)
                n = chunk_tiles(c) * P
                act.wait_ge(a_ld[u % RING], 16 * (u // RING + 1))
                if u >= RING:
                    wait_unit(act, u - RING)
                act.activation(a_hi[:, u % RING, 0:n], a_raw[:, u % RING, 0:n], ACT.Copy).then_inc(a_hi_done, 1)
                if u == first_unit[1]:
                    act.wait_ge(w_ld, 32)
                    act.activation(w_hi[:, :, :], w_raw[:, :, :], ACT.Copy).then_inc(w_hi_done, 1)
                    act.activation(gw1_hi[:, :, :], gw1_raw[:, :, :], ACT.Copy).then_inc(w_hi_done, 1)
            finish(post)
            act.wait_ge(phase1, 2)

            def w1_split(s, m, first):
                act.wait_ge(w1_ld[m], 16 * s + 16)
                if not first:
                    act.wait_ge(h_ready, HC * (s - 1) + 2 * m + 2)
                act.activation(w1_hi[:, :, m * 256:(m + 1) * 256], w1_raw[:, :, m * 256:(m + 1) * 256],
                               ACT.Copy).then_inc(w1_hi_done, 1)

            def w2_split(s, m, first):
                act.wait_ge(w2_ld[m], 16 * s + 16)
                if not first:
                    if m < 3:
                        act.wait_ge(w2_used, 3 * (s - 1) + m + 1)
                    else:
                        act.wait_ge(ye_ready, SJ * s)
                act.activation(w2_hi[:, 2 * m:2 * m + 2, :], w2_raw[:, 2 * m:2 * m + 2, :],
                               ACT.Copy).then_inc(w2_hi_done, 1)

            def xe_split(s):
                for jj in range(SJ):
                    act.wait_ge(xe_ready, SJ * s + jj + 1)
                    act.activation(xe_hi[:, :, jj * P:(jj + 1) * P],
                                   bank[jj][:, :].rearrange("p (c n) -> p c n", c=DC),
                                   ACT.Copy).then_inc(xe_hi_done, 1)

            def step(s, nxt):
                act.wait_ge(be1_ld, 16 * s + 16)
                for m in range(4):
                    hb = bank[2 + m]
                    act.wait_ge(h_ready, HC * s + 2 * m + 2)
                    for k in range(2):
                        act.activation(hb[:, k * 256:(k + 1) * 256], hb[:, k * 256:(k + 1) * 256], ACT.Gelu,
                                       bias=be1_sb[:, 2 * m + k:2 * m + k + 1]).then_inc(gelu_done, 1)
                    act.wait_ge(gelu_done, HC * s + 2 * m + 2)
                    act.activation(h_hi[:, 2 * m:2 * m + 2, :], hb[:, :].rearrange("p (k n) -> p k n", k=2),
                                   ACT.Copy).then_inc(h_hi_done, 1)
                    if nxt:
                        w1_split(s + 1, m, False)
                if nxt:
                    xe_split(s + 1)
                    for m in range(4):
                        w2_split(s + 1, m, False)

            for m in range(4):
                w1_split(0, m, True)
            xe_split(0)
            for m in range(4):
                w2_split(0, m, True)
            step(0, True)
            with act.Fori(1, STEPS - 1) as s:
                step(s, True)
            step(STEPS - 1, False)

        @block.vector
        def _(dve):
            own = [0]

            def link(ins):
                own[0] += 1
                ins.then_inc(dve_own, 1)
                dve.wait_ge(dve_own, own[0])

            dve.wait_ge(consts, 1)
            link(dve.tensor_scalar(pre[:, :, 0], pre[:, :, 0], S_ROWS - 1, None, ALU.bitwise_and))
            link(dve.tensor_scalar(pre[:, :, 0], pre[:, :, 0], float(DUMMY), None, ALU.add))
            link(dve.memset(pre[:, :, 1], 0))
            dve.nop().then_inc(pre_rdy, 1)
            link(dve.tensor_copy(base[:, :], base0[:, :]))
            dve.wait_ge(const_ld, 48)

            def stats(j):
                dve.wait_ge(x_ld[j % 2], 16 * (j // 2 + 1))
                link(dve.bn_stats(stat6[:, j % 2, :], x_in[:, j % 2, :]))
                dve.bn_aggr(mv[:, j, :], stat6[:, j % 2, :]).then_inc(mv_done, 1)

            def xs_make(j):
                dve.wait_ge(scl_done, j + 1)
                dve.wait_ge(mv_done, j + 1)
                if j >= 2:
                    dve.wait_ge(xs_lo_done, j - 1)
                dve.tensor_scalar(x_n[:, j % 2, :], x_in[:, j % 2, :], mv[:, j, 0:1], scl[:, j:j + 1],
                                  ALU.subtract, ALU.mult).then_inc(xn_done, 1)

            def xs_rest(j):
                dve.wait_ge(xs_hi_done, j + 1)
                dve.tensor_tensor(xs_lo[:, j, :], x_n[:, j % 2, :], xs_hi[:, j, :].bitcast(F32),
                                  ALU.subtract).then_inc(xs_lo_done, 1)

            def evac_m(c):
                for i in range(chunk_tiles(c)):
                    t = c * CT + i
                    dve.wait_ge(m_ready, t + 1)
                    if c == 0 and i == 0:
                        dve.wait_ge(pre_st, 48)
                    if c >= 2:
                        dve.wait_ge(mt_ready, t - 2 * CT + 1)
                    g = max(c - 1, 0)
                    dve.tensor_tensor(m_raw[:, c % 2, i, :], bank_of(g, c, i)[:, :],
                                      xs_hi[:, t, :].bitcast(F32), ALU.add).then_inc(m_evac, 1)

            def mt_rest(p):
                for q in range(2):
                    dve.wait_ge(mt_hi_done, 2 * p + q + 1)
                    dve.tensor_tensor(mt_lo[:, q, :, :], bank[BY + q][:, :].rearrange("p (c n) -> p c n", c=DC),
                                      mt_hi[:, q, :, :].bitcast(F32), ALU.subtract).then_inc(mt_lo_done, 1)

            def neg_part(p, q):
                t = 2 * p + q
                dve.wait_ge(y_ready, t + 1)
                dve.tensor_scalar(e_buf[:, q, :], bank[BY + q][:, :], dinv(t), 0.0,
                                  ALU.mult, ALU.min).then_inc(neg_done, 1)

            def elu_norm(p, qs):
                for q in qs:
                    t = 2 * p + q
                    dve.wait_ge(exp_done, t + 1)
                    link(dve.tensor_scalar(e_buf[:, q, :], e_buf[:, q, :], -1.0, None, ALU.add))
                    link(dve.scalar_tensor_tensor(e_buf[:, q, :], bank[BY + q][:, :], dinv(t), e_buf[:, q, :],
                                                  ALU.mult, ALU.max))
                    dve.wait_ge(x_ld[q], 16 * (NT // 2 + p + 1))
                    link(dve.tensor_tensor(x_in[:, q, :], e_buf[:, q, :], x_in[:, q, :], ALU.add))
                    link(dve.bn_stats(stat6[:, q, :], x_in[:, q, :]))
                    dve.bn_aggr(mv2[:, q, :], stat6[:, q, :]).then_inc(mv2_done, 1)
                for q in qs:
                    t = 2 * p + q
                    dve.wait_ge(rstd2_done, t + 1)
                    dve.wait_ge(mv2_done, t + 1)
                    if p > 0:
                        dve.wait_ge(xln_st[q], 16 * p)
                    dve.tensor_scalar(x_n[:, q, :], x_in[:, q, :], mv2[:, q, 0:1], rstd2[:, q, :],
                                      ALU.subtract, ALU.mult).then_inc(xl_done, 1)

            def xt_rest(p):
                for q in range(2):
                    dve.wait_ge(xt_hi_done, 2 * p + q + 1)
                    dve.tensor_tensor(xt_lo[:, :, q * P:(q + 1) * P],
                                      bank[BY + q][:, :].rearrange("p (c n) -> p c n", c=DC),
                                      xt_hi[:, :, q * P:(q + 1) * P].bitcast(F32),
                                      ALU.subtract).then_inc(xt_lo_done, 1)

            def experts(p):
                dve.wait_ge(l_ready, p + 1)
                link(dve.tensor_tensor(lg[:, :, :], bank[BS][:, L_AT:L_AT + 2 * E].rearrange("p (q e) -> p q e", q=2),
                                       gb2_sb[:, :].unsqueeze(1).to_broadcast([P, 2, E]), ALU.add))
                link(dve.tensor_reduce(lmax[:, :], lg[:, :, :], AX.X, ALU.max))
                dve.tensor_tensor(lc[:, :, :], lg[:, :, :], lmax[:, :].unsqueeze(2).to_broadcast([P, 2, E]),
                                  ALU.subtract).then_inc(lc_done, 1)
                dve.wait_ge(le_done, p + 1)
                link(dve.tensor_reduce(lsum[:, :], le[:, :, :], AX.X, ALU.add))
                link(dve.reciprocal(lrec[:, :], lsum[:, :]))
                link(dve.tensor_tensor(prob[:, :, :], le[:, :, :], lrec[:, :].unsqueeze(2).to_broadcast([P, 2, E]),
                                       ALU.mult))
                for q in range(2):
                    link(dve.max(top[:, q, :], prob[:, q, :]))
                dve.tensor_tensor(pd[:, :], top[:, :, 1], top[:, :, 0], ALU.subtract).then_inc(pd_done, 1)
                for q in range(2):
                    link(dve.max_index(topi[:, q, :], top[:, q, :], prob[:, q, :]))
                link(dve.tensor_copy(topf[:, :, :], topi[:, :, :]))
                for q in range(2):
                    for k in range(TOP_K):
                        link(dve.tensor_scalar(hot[:, q, k, :], cols8[:, :], topf[:, q, k:k + 1], None, ALU.is_equal))
                dve.tensor_tensor(mask[:, :, :], hot[:, :, 0, :], hot[:, :, 1, :], ALU.add).then_inc(mask_done, 1)
                dve.wait_ge(pe2_done, p + 1)
                link(dve.tensor_scalar(pden[:, :], pe2[:, :], 1.0, None, ALU.add))
                link(dve.reciprocal(wts[:, :, 0], pden[:, :]))
                link(dve.tensor_tensor(wts[:, :, 1], wts[:, :, 0], pe2[:, :], ALU.mult))

            def slots(p):
                b = p % 2
                dve.wait_ge(r_ready, p + 1)
                link(dve.tensor_tensor(rb[:, :, :], bank[BS][:, R_AT:R_AT + 2 * E].rearrange("p (q e) -> p q e", q=2),
                                       base[:, :].unsqueeze(1).to_broadcast([P, 2, E]), ALU.add))
                link(dve.tensor_tensor(pick[:, :, :, :], hot[:, :, :, :],
                                       rb[:, :, :].unsqueeze(2).to_broadcast([P, 2, TOP_K, E]), ALU.mult))
                link(dve.tensor_reduce(slotf[:, :, :], pick[:, :, :, :], AX.X, ALU.add))
                if p >= 2:
                    dve.wait_ge(list_st, 16 * 2 * TOP_K * (p - 1))
                link(dve.tensor_copy(slot[:, b, :, :], slotf[:, :, :]))
                link(dve.tensor_copy(pay[:, b, :, :, 0],
                                     tok_id[:, 2 * p:2 * p + 2].unsqueeze(2).to_broadcast([P, 2, TOP_K])))
                link(dve.tensor_copy(pay[:, b, :, :, 1].bitcast(F32), wts[:, :, :]))
                dve.tensor_tensor(base[:, :], base[:, :], bank[BS][:, C_AT:C_AT + E], ALU.add).then_inc(route_done, 1)
                dve.wait_ge(route_done, p + 1)

            post = events([("mt", mt_rest), ("y0", lambda p: neg_part(p, 0)), ("y1", lambda p: neg_part(p, 1)),
                           ("y1", lambda p: elu_norm(p, (0, 1))), ("xt", xt_rest),
                           ("logit", experts), ("rank", slots)], REACT)
            evac = {}
            for c in range(NCH):
                g = max(c - 1, 0)
                evac.setdefault(first_unit.get(g + 1, NU) + 1, []).append(c)
            stats(0)
            for u, (g, j, c) in enumerate(units):
                if g == 0 and c == 0:
                    if j + 1 < NT:
                        stats(j + 1)
                    xs_make(j)
                    xs_rest(j)
                run(post, u)
                for cc in evac.pop(u, ()):
                    evac_m(cc)
                n = chunk_tiles(c) * P
                dve.wait_ge(a_hi_done, u + 1)
                dve.tensor_tensor(a_lo[:, u % RING, 0:n], a_raw[:, u % RING, 0:n],
                                  a_hi[:, u % RING, 0:n].bitcast(F32), ALU.subtract).then_inc(a_lo_done, 1)
                if u == first_unit[1]:
                    dve.wait_ge(w_hi_done, 2)
                    dve.tensor_tensor(w_lo[:, :, :], w_raw[:, :, :], w_hi[:, :, :].bitcast(F32),
                                      ALU.subtract).then_inc(w_lo_done, 1)
                    dve.tensor_tensor(gw1_lo[:, :, :], gw1_raw[:, :, :], gw1_hi[:, :, :].bitcast(F32),
                                      ALU.subtract).then_inc(w_lo_done, 1)
            for k in sorted(evac):
                for cc in evac[k]:
                    evac_m(cc)
            finish(post)

            link(dve.tensor_tensor(cnt[:, :], base[:, :], base0[:, :], ALU.subtract))
            link(dve.tensor_scalar(tiles_i[:, :], cnt[:, :], float(S_ROWS - 1), None, ALU.add))
            link(dve.tensor_scalar(tiles_i[:, :], tiles_i[:, :], S_ROWS.bit_length() - 1, None,
                                   ALU.logical_shift_right))
            link(dve.tensor_copy(tiles_f[:, :], tiles_i[:, :]))
            link(dve.tensor_copy(cum[:, 0, :], tiles_f[:, :]))
            for n, d in enumerate((1, 2, 4)):
                link(dve.tensor_copy(cum[:, n + 1, 0:d], cum[:, n, 0:d]))
                link(dve.tensor_tensor(cum[:, n + 1, d:E], cum[:, n, d:E], cum[:, n, 0:E - d], ALU.add))
            link(dve.tensor_tensor(past[:, :, :], cum[:, 3, :].unsqueeze(1).to_broadcast([P, STEPS, E]),
                                   s_i[:, :].unsqueeze(2).to_broadcast([P, STEPS, E]), ALU.is_le))
            link(dve.tensor_tensor(past_t[:, :, :], past[:, :, :],
                                   tiles_f[:, :].unsqueeze(1).to_broadcast([P, STEPS, E]), ALU.mult))
            link(dve.tensor_reduce(s_e[:, :], past[:, :, :], AX.X, ALU.add))
            link(dve.tensor_reduce(s_t[:, :], past_t[:, :, :], AX.X, ALU.add))
            link(dve.tensor_tensor(s_t[:, :], s_i[:, :], s_t[:, :], ALU.subtract))
            link(dve.tensor_scalar(s_t[:, :], s_t[:, :], float(S_ROWS), None, ALU.mult))
            link(dve.tensor_scalar(s_r[:, :, 1], s_e[:, :], float(E - 1), None, ALU.min))
            link(dve.tensor_scalar(s_r[:, :, 0], s_e[:, :], float(CAP), None, ALU.mult))
            link(dve.tensor_tensor(s_r[:, :, 0], s_r[:, :, 0], s_t[:, :], ALU.add))
            dve.tensor_copy(sched[:, :, :], s_r[:, :, :]).then_inc(phase1, 1)
            dve.wait_ge(phase1, 2)

            def w1_rest(s, m):
                dve.wait_ge(w1_hi_done, 4 * s + m + 1)
                dve.tensor_tensor(w1_lo[:, :, m * 256:(m + 1) * 256], w1_raw[:, :, m * 256:(m + 1) * 256],
                                  w1_hi[:, :, m * 256:(m + 1) * 256].bitcast(F32),
                                  ALU.subtract).then_inc(w1_lo_done, 1)

            def w2_rest(s, m):
                dve.wait_ge(w2_hi_done, 4 * s + m + 1)
                dve.tensor_tensor(w2_lo[:, 2 * m:2 * m + 2, :], w2_raw[:, 2 * m:2 * m + 2, :],
                                  w2_hi[:, 2 * m:2 * m + 2, :].bitcast(F32),
                                  ALU.subtract).then_inc(w2_lo_done, 1)

            def xe_rest(s):
                for jj in range(SJ):
                    dve.wait_ge(xe_hi_done, SJ * s + jj + 1)
                    dve.tensor_tensor(xe_lo[:, :, jj * P:(jj + 1) * P],
                                      bank[jj][:, :].rearrange("p (c n) -> p c n", c=DC),
                                      xe_hi[:, :, jj * P:(jj + 1) * P].bitcast(F32),
                                      ALU.subtract).then_inc(xe_lo_done, 1)

            def weigh(s, first):
                dve.wait_ge(be2_ld, 16 * s + 16)
                dve.wait_ge(ly_ld, 16 * s + 16)
                for jj in range(SJ):
                    dve.wait_ge(ye_ready, SJ * s + jj + 1)
                    if not first:
                        dve.wait_ge(y_add, 16 * (SJ * (s - 1) + jj + 1))
                    dve.tensor_tensor(y_sb[:, jj, :], bank[6 + jj][:, :], be2_sb[:, :], ALU.add).then_inc(yb_done, 1)
                    dve.wait_ge(yb_done, SJ * s + jj + 1)
                    dve.tensor_scalar(y_sb[:, jj, :], y_sb[:, jj, :], list_y[:, jj, 1:2].bitcast(F32), None,
                                      ALU.mult).then_inc(yw_done, 1)

            def step(s, nxt, earlier):
                for m in range(4):
                    dve.wait_ge(h_hi_done, 4 * s + m + 1)
                    dve.tensor_tensor(h_lo[:, 2 * m:2 * m + 2, :], bank[2 + m][:, :].rearrange("p (k n) -> p k n", k=2),
                                      h_hi[:, 2 * m:2 * m + 2, :].bitcast(F32), ALU.subtract).then_inc(h_lo_done, 1)
                    if m == 0 and earlier > 0:
                        weigh(s - 1, earlier == 1)
                    if nxt:
                        w1_rest(s + 1, m)
                if nxt:
                    xe_rest(s + 1)
                    for m in range(4):
                        w2_rest(s + 1, m)

            for m in range(4):
                w1_rest(0, m)
            xe_rest(0)
            for m in range(4):
                w2_rest(0, m)
            step(0, True, 0)
            step(1, True, 1)
            with dve.Fori(2, STEPS - 1) as s:
                step(s, True, 2)
            step(STEPS - 1, False, 2)
            weigh(STEPS - 1, False)

        @block.tensor
        def _(pe):
            def three(dst, a_h, a_l, b_h, b_l, start, stop):
                pe.matmul(dst, a_h, b_h, start=start, stop=False)
                pe.matmul(dst, a_h, b_l, start=False, stop=False)
                return pe.matmul(dst, a_l, b_h, start=False, stop=stop)

            def transpose_m(p):
                for q in range(2):
                    t = 2 * p + q
                    c, i = t // CT, t % CT
                    pe.wait_ge(m_full, t + 1)
                    if p == 0:
                        pe.wait_ge(m_evac, 2 * CT)
                    else:
                        pe.wait_ge(xt_lo_done, t - 1)
                    for d in range(DC):
                        last = pe.transpose(bank[BY + q][:, d * P:(d + 1) * P],
                                            m_raw[:, c % 2, i, d * P:(d + 1) * P], ident[:, :])
                    last.then_inc(mt_ready, 1)

            def project(p, q):
                t = 2 * p + q
                pe.wait_ge(mt_lo_done, t + 1)
                pe.wait_ge(w_lo_done, 2)
                for d in range(DC):
                    last = three(bank[BY + q][:, :], mt_hi[:, q, d, :], mt_lo[:, q, d, :],
                                 w_hi[:, d, :], w_lo[:, d, :], d == 0, d == DC - 1)
                last.then_inc(y_ready, 1)

            def transpose_x(p):
                for q in range(2):
                    pe.wait_ge(xl_done, 2 * p + q + 1)
                    for d in range(DC):
                        last = pe.transpose(bank[BY + q][:, d * P:(d + 1) * P], x_n[:, q, d * P:(d + 1) * P],
                                            ident[:, :])
                    last.then_inc(xt_ready, 1)

            def gate(p):
                pe.wait_ge(xt_lo_done, 2 * p + 2)
                if p > 0:
                    pe.wait_ge(g_done, GC * p)
                for hb in range(GC):
                    for d in range(DC):
                        last = three(bank[BG][:, hb * 256:(hb + 1) * 256],
                                     gw1_hi[:, d, hb * P:(hb + 1) * P], gw1_lo[:, d, hb * P:(hb + 1) * P],
                                     xt_hi[:, d, :], xt_lo[:, d, :], d == 0, d == DC - 1)
                last.then_inc(g_ready, 1)

            def logits(p):
                pe.wait_ge(g_done, GC * (p + 1))
                if p > 0:
                    pe.wait_ge(route_done, p)
                for q in range(2):
                    for hb in range(GC):
                        last = pe.matmul(bank[BS][:, L_AT + q * E:L_AT + (q + 1) * E], g_t[:, hb, q * P:(q + 1) * P],
                                         gw2_sb[:, hb, :], start=hb == 0, stop=hb == GC - 1)
                last.then_inc(l_ready, 1)

            def ranks(p):
                pe.wait_ge(mask_done, p + 1)
                r = bank[BS]
                pe.matmul(r[:, R_AT:R_AT + E], upper[:, :], mask[:, 0, :], start=True, stop=True)
                pe.matmul(r[:, R_AT + E:R_AT + 2 * E], upper[:, :], mask[:, 1, :], start=True, stop=False)
                pe.matmul(r[:, R_AT + E:R_AT + 2 * E], ones_bf[:, :], mask[:, 0, :], start=False, stop=True)
                pe.matmul(r[:, C_AT:C_AT + E], ones_bf[:, :], mask[:, 0, :], start=True, stop=False)
                pe.matmul(r[:, C_AT:C_AT + E], ones_bf[:, :], mask[:, 1, :], start=False,
                          stop=True).then_inc(r_ready, 1)

            post = events([("mt", transpose_m), ("y0", lambda p: project(p, 0)), ("y1", lambda p: project(p, 1)),
                           ("xt", transpose_x), ("gate", gate), ("logit", logits), ("rank", ranks)], 0)
            pe.wait_ge(consts, 1)
            for u, (g, j, c) in enumerate(units):
                if c == 0:
                    pe.wait_ge(xs_lo_done, j + 1)
                pe.wait_ge(a_lo_done, u + 1)
                k = u % RING
                for i in range(chunk_tiles(c)):
                    if j == 0 and g > 0:
                        before = 0 if g == 1 else g
                        pe.wait_ge(m_evac, before * CT + i + 1)
                    last = three(bank_of(g, c, i)[:, :], a_hi[:, k, i * P:(i + 1) * P], a_lo[:, k, i * P:(i + 1) * P],
                                 xs_hi[:, j, :], xs_lo[:, j, :], j == 0, j == NT - 1)
                    if j == NT - 1:
                        last.then_inc(m_ready, 1)
                if j < NT - 1:
                    last.then_inc(unit_done, 1)
                run(post, u)
            finish(post)
            pe.wait_ge(phase1, 2)

            def transpose_xe(s, first):
                if not first:
                    pe.wait_ge(xe_lo_done, SJ * s)
                for jj in range(SJ):
                    pe.wait_ge(xg_ld, 16 * (SJ * s + SJ))
                    for d in range(DC):
                        last = pe.transpose(bank[jj][:, d * P:(d + 1) * P], x_g[:, jj, d * P:(d + 1) * P],
                                            ident[:, :])
                    last.then_inc(xe_ready, 1)

            def step(s, nxt, first):
                pe.wait_ge(xe_lo_done, SJ * s + SJ)
                for k in range(HC):
                    if k % 2 == 0:
                        pe.wait_ge(w1_lo_done, 4 * s + k // 2 + 1)
                        if not first:
                            pe.wait_ge(h_lo_done, 4 * (s - 1) + k // 2 + 1)
                    for d in range(DC):
                        last = three(bank[2 + k // 2][:, k % 2 * 256:k % 2 * 256 + 256],
                                     w1_hi[:, d, k * P:(k + 1) * P], w1_lo[:, d, k * P:(k + 1) * P],
                                     xe_hi[:, d, :], xe_lo[:, d, :], d == 0, d == DC - 1)
                    last.then_inc(h_ready, 1)
                if nxt:
                    transpose_xe(s + 1, False)
                if not first:
                    pe.wait_ge(yw_done, SJ * s)
                for k in range(HC):
                    if k % 2 == 0:
                        pe.wait_ge(w2_lo_done, 4 * s + k // 2 + 1)
                        pe.wait_ge(h_lo_done, 4 * s + k // 2 + 1)
                    for jj in range(SJ):
                        last = three(bank[6 + jj][:, :], h_hi[:, k, jj * P:(jj + 1) * P], h_lo[:, k, jj * P:(jj + 1) * P],
                                     w2_hi[:, k, :], w2_lo[:, k, :], k == 0, k == HC - 1)
                        if k == HC - 1:
                            last.then_inc(ye_ready, 1)
                        elif k % 2 and jj == SJ - 1:
                            last.then_inc(w2_used, 1)

            transpose_xe(0, True)
            step(0, True, True)
            with pe.Fori(1, STEPS - 1) as s:
                step(s, True, False)
            step(STEPS - 1, False, False)


def kernel(x, adj, L0_gnn_w, L0_ffn_gw1, L0_ffn_gb1, L0_ffn_gw2, L0_ffn_gb2, L0_ffn_we1, L0_ffn_be1,
           L0_ffn_we2, L0_ffn_be2):
    import numpy as np
    import concourse.bacc as bacc
    from concourse import mybir as mb
    from concourse.bass_utils import run_bass_kernel_spmd

    x_p = np.zeros((NP, D), np.float32)
    x_p[:N_TOK] = np.asarray(x)
    a_p = np.zeros((NP, NP), np.float32)
    a_p[:N_TOK, :N_TOK] = np.asarray(adj)
    arrays = {
        "x_in": x_p,
        "adj_in": a_p,
        "adj_t_in": np.ascontiguousarray(a_p.T),
        "w_in": np.ascontiguousarray(L0_gnn_w),
        "gw1_in": np.ascontiguousarray(L0_ffn_gw1),
        "gb1_in": np.ascontiguousarray(np.asarray(L0_ffn_gb1).reshape(GC, P).T),
        "gw2_in": np.ascontiguousarray(L0_ffn_gw2),
        "gb2_in": np.ascontiguousarray(L0_ffn_gb2),
        "we1_in": np.ascontiguousarray(L0_ffn_we1),
        "be1_in": np.ascontiguousarray(np.asarray(L0_ffn_be1).reshape(E, HC, P).transpose(0, 2, 1)),
        "we2_in": np.ascontiguousarray(L0_ffn_we2),
        "be2_in": np.ascontiguousarray(L0_ffn_be2),
    }
    nc = bacc.Bacc("TRN2", target_bir_lowering=False, num_devices=1)
    args = [nc.dram_tensor(n, a.shape, mb.dt.from_np(a.dtype), kind="ExternalInput").ap() for n, a in arrays.items()]
    args.append(nc.dram_tensor("out_rows", (ROWS, D), F32, kind="ExternalOutput").ap())
    build(nc, *args)
    r = run_bass_kernel_spmd(nc, [arrays], core_ids=[0])
    return r.results[0]["out_rows"][:N_TOK]
```

```python
import concourse.bass as bass
from concourse import mybir
from contextlib import ExitStack

F32 = mybir.dt.float32
F32R = mybir.dt.float32r
BF16 = mybir.dt.bfloat16
I32 = mybir.dt.int32
U32 = mybir.dt.uint32
ALU = mybir.AluOpType
ACT = mybir.ActivationFunctionType
AX = mybir.AxisListType

P = 128
N_TOK = 3327
NT = -(-N_TOK // P)
NP = NT * P
D = 512
DC = D // P
GH = 256
GC = GH // P
E = 8
H = 1024
HC = H // P
TOP_K = 2
EPS = 1e-5

S_ROWS = 256
SJ = S_ROWS // P
CAP = -(-NP // S_ROWS) * S_ROWS
STEPS = (TOP_K * NP + E * (S_ROWS - 1)) // S_ROWS
DUMMY = NP
ROWS = NP + S_ROWS
SLOTS = (E + 1) * CAP

CW = 512
CT = CW // P
NCH = -(-NP // CW)
RING = 4


def build(nc, x, adj, adj_t, w, gw1, gb1, gw2, gb2, we1, be1, we2, be2, out):
    ctx = ExitStack()
    with ctx:
        arena = [-(-nc.sbuf_base // 32) * 32]

        def at(name, shape, dt):
            n = 1
            for k in shape[1:]:
                n *= k
            size = -(-n * (2 if dt == BF16 else 4) // 32) * 32
            t = nc.alloc_sbuf_tensor_at(name, shape, dt, offset=arena[0])
            arena[0] += size
            return t

        def sem(name):
            return ctx.enter_context(nc.semaphore(name))

        ident = at("ident", [P, P], F32)
        ones = at("ones", [P, P], F32)
        upper = at("upper", [P, P], BF16)
        ones_bf = at("ones_bf", [P, P], BF16)
        ln_add = at("ln_add", [P, 2], F32)
        ln_pow = at("ln_pow", [P, 2], F32)
        sched = at("sched", [P, STEPS, 2], I32)
        cols8 = at("cols8", [P, E], F32)
        tok_id = at("tok_id", [P, NT], I32)
        base0 = at("base0", [P, E], F32)
        base = at("base", [P, E], F32)
        common_end = arena[0]

        xs_hi = at("xs_hi", [P, NT, D], F32R)
        xs_lo = at("xs_lo", [P, NT, D], F32R)
        xs_end = arena[0]
        a_raw = at("a_raw", [P, RING, CW], F32)
        a_hi = at("a_hi", [P, RING, CW], F32R)
        a_lo = at("a_lo", [P, RING, CW], F32R)
        m_at = arena[0]
        m_raw = at("m_raw", [P, 3, CT, D], F32)
        mt_hi = at("mt_hi", [P, DC, P], F32R)
        mt_lo = at("mt_lo", [P, DC, P], F32R)
        x_in = at("x_in", [P, 2, D], F32)
        x_n = at("x_n", [P, 2, D], F32)
        stat6 = at("stat6", [P, 2, 6], F32)
        mv = at("mv", [P, NT, 2], F32)
        pk = at("pk", [P, 2, 2], F32)
        rs = at("rs", [P, NT, 2], F32)
        scl = at("scl", [P, NT], F32)
        deg = at("deg", [P, NT, 2], F32)
        deg1 = at("deg1", [P, 2, 1], F32)
        gb1_sb = at("gb1_sb", [P, GC], F32)
        gw2_sb = at("gw2_sb", [P, GC, E], F32)
        gb2_sb = at("gb2_sb", [P, E], F32)
        mv2 = at("mv2", [P, 2, 2], F32)
        pk2 = at("pk2", [P, 2, 1], F32)
        rstd2 = at("rstd2", [P, 2, 1], F32)
        lg = at("lg", [P, 2, E], F32)
        lmax = at("lmax", [P, 2], F32)
        lc = at("lc", [P, 2, E], F32)
        le = at("le", [P, 2, E], F32)
        lsum = at("lsum", [P, 2], F32)
        lrec = at("lrec", [P, 2], F32)
        prob = at("prob", [P, 2, E], F32)
        top = at("top", [P, 2, 8], F32)
        topi = at("topi", [P, 2, 8], U32)
        topf = at("topf", [P, 2, 8], F32)
        hot = at("hot", [P, 2, TOP_K, E], F32)
        mask = at("mask", [P, 2, E], BF16)
        pd = at("pd", [P, 2], F32)
        pe2 = at("pe2", [P, 2], F32)
        pden = at("pden", [P, 2], F32)
        wts = at("wts", [P, 2, TOP_K], F32)
        rb = at("rb", [P, 2, E], F32)
        pick = at("pick", [P, 2, TOP_K, E], F32)
        slotf = at("slotf", [P, 2, TOP_K], F32)
        slot = at("slot", [P, 2, 2, TOP_K], I32)
        pay = at("pay", [P, 2, 2, TOP_K, 2], I32)
        cnt = at("cnt", [P, E], F32)
        tiles_i = at("tiles_i", [P, E], I32)
        tiles_f = at("tiles_f", [P, E], F32)
        cum = at("cum", [P, 4, E], F32)
        s_i = at("s_i", [P, STEPS], F32)
        past = at("past", [P, STEPS, E], F32)
        past_t = at("past_t", [P, STEPS, E], F32)
        s_e = at("s_e", [P, STEPS], F32)
        s_t = at("s_t", [P, STEPS], F32)
        s_r = at("s_r", [P, STEPS, 2], F32)
        HALF = NP // 2
        shared = arena[0]
        row_in = at("row_in", [P, 3, HALF], F32)
        late_at = arena[0] = max(arena[0], shared + (2 * DC * D + DC * GH) * 4)
        m_late = at("m_late", [P, CT, D], F32)
        late_end = arena[0]

        def over(name, shape, dt, place):
            return nc.alloc_sbuf_tensor_at(name, shape, dt, offset=place)

        arena[0] = shared
        w_raw = over("w_raw", [P, DC, D], F32, arena[0])
        w_lo = at("w_lo", [P, DC, D], F32R)
        gw1_raw = over("gw1_raw", [P, DC, GH], F32, arena[0])
        gw1_lo = at("gw1_lo", [P, DC, GH], F32R)
        w_hi = at("w_hi", [P, DC, D], F32R)
        arena[0] = late_at
        xt_hi = at("xt_hi", [P, DC, 2 * P], F32R)
        xt_lo = at("xt_lo", [P, DC, 2 * P], F32R)
        arena[0] = max(arena[0], late_end)
        gw1_hi = at("gw1_hi", [P, DC, GH], F32R)
        g_t = at("g_t", [P, GC, 2 * P], F32)

        PRE = SLOTS // P
        pre = over("pre", [P, PRE, 2], I32, m_at)
        zrow = over("zrow", [P, SJ, D], F32, m_at + CT * D * 4)

        arena[0] = common_end
        w1_raw = at("w1_raw", [P, DC, H], F32)
        w2_raw = at("w2_raw", [P, HC, D], F32)
        w1_hi = at("w1_hi", [P, DC, H], F32R)
        w1_lo = at("w1_lo", [P, DC, H], F32R)
        w2_hi = at("w2_hi", [P, HC, D], F32R)
        w2_lo = at("w2_lo", [P, HC, D], F32R)
        x_g = at("x_g", [P, SJ, D], F32)
        xe_hi = at("xe_hi", [P, DC, S_ROWS], F32R)
        xe_lo = at("xe_lo", [P, DC, S_ROWS], F32R)
        h_hi = at("h_hi", [P, HC, S_ROWS], F32R)
        h_lo = at("h_lo", [P, HC, S_ROWS], F32R)
        y_sb = at("y_sb", [P, SJ, D], F32)
        be1_sb = at("be1_sb", [P, HC], F32)
        be2_sb = at("be2_sb", [P, D], F32)
        list_g = at("list_g", [P, SJ, 2], I32)
        list_y = at("list_y", [P, SJ, 2], I32)

        bank = [ctx.enter_context(nc.psum_tensor(f"bank{b}", [P, 512], F32)) for b in range(8)]
        BY, BG, BS = 4, 6, 7
        L_AT, R_AT, C_AT = 0, 32, 64

        m_dram = nc.dram_tensor("m_dram", (P, CT, D), F32).ap()
        xln = nc.dram_tensor("xln", (ROWS, D), F32).ap()
        lists = nc.dram_tensor("lists", (SLOTS, 2), I32).ap()

        consts = sem("consts")
        const_ld = sem("const_ld")
        w_ld = sem("w_ld")
        a_ld = [sem(f"a_ld{i}") for i in range(RING)]
        x_ld = [sem(f"x_ld{i}") for i in range(2)]
        row_ld = [sem(f"row_ld{i}") for i in range(3)]
        pre_st = sem("pre_st")
        pre_rdy = sem("pre_rdy")
        deg_done = sem("deg_done")
        mv_done = sem("mv_done")
        scl_done = sem("scl_done")
        xn_done = sem("xn_done")
        xs_hi_done = sem("xs_hi_done")
        xs_lo_done = sem("xs_lo_done")
        a_hi_done = sem("a_hi_done")
        a_lo_done = sem("a_lo_done")
        unit_done = sem("unit_done")
        bank_full = sem("bank_full")
        bank_read = sem("bank_read")
        late_st = sem("late_st")
        late_ld = sem("late_ld")
        m_full = sem("m_full")
        w_hi_done = sem("w_hi_done")
        w_lo_done = sem("w_lo_done")
        mt_ready = sem("mt_ready")
        mt_hi_done = sem("mt_hi_done")
        mt_lo_done = sem("mt_lo_done")
        y_ready = sem("y_ready")
        neg_done = sem("neg_done")
        exp_done = sem("exp_done")
        x1_done = sem("x1_done")
        mv2_done = sem("mv2_done")
        rstd2_done = sem("rstd2_done")
        xl_done = sem("xl_done")
        x1_st = [sem(f"x1_st{i}") for i in range(2)]
        xln_st = [sem(f"xln_st{i}") for i in range(2)]
        xt_ready = sem("xt_ready")
        xt_hi_done = sem("xt_hi_done")
        xt_lo_done = sem("xt_lo_done")
        g_ready = sem("g_ready")
        g_done = sem("g_done")
        l_ready = sem("l_ready")
        lc_done = sem("lc_done")
        le_done = sem("le_done")
        pd_done = sem("pd_done")
        pe2_done = sem("pe2_done")
        mask_done = sem("mask_done")
        r_ready = sem("r_ready")
        route_done = sem("route_done")
        list_st = [sem(f"list_st{q}") for q in range(2)]
        sched_done = sem("sched_done")
        dve_own = sem("dve_own")
        pool_own = sem("pool_own")
        phase1 = sem("phase1")
        lg_ld = sem("lg_ld")
        ly_ld = sem("ly_ld")
        w1_ld = [sem(f"w1_ld{i}") for i in range(4)]
        w2_ld = [sem(f"w2_ld{i}") for i in range(4)]
        be1_ld = sem("be1_ld")
        be2_ld = sem("be2_ld")
        xg_ld = sem("xg_ld")
        xe_ready = sem("xe_ready")
        xe_hi_done = sem("xe_hi_done")
        xe_lo_done = sem("xe_lo_done")
        w1_hi_done = sem("w1_hi_done")
        w1_lo_done = sem("w1_lo_done")
        w2_hi_done = sem("w2_hi_done")
        w2_lo_done = sem("w2_lo_done")
        h_ready = sem("h_ready")
        gelu_done = sem("gelu_done")
        h_hi_done = sem("h_hi_done")
        h_lo_done = sem("h_lo_done")
        w2_used = sem("w2_used")
        ye_ready = sem("ye_ready")
        yb_done = sem("yb_done")
        yw_done = sem("yw_done")
        y_add = sem("y_add")
        waited = sem("waited")

        LATE = 3
        M_AT = {0: 0, 1: 1, 2: 2, LATE: 1, 4: 0, 5: 2, 6: 0}
        turns = [((2, 3), 0, 3), ((0, 1), 0, 6), ((2, 3), 3, 9), ((0, 1), 6, 12), ((2, 3), 9, 15),
                 ((0, 1), 12, 18), ((2, 3), 15, 21), ((0, 1), 18, NT), ((2, 3), 21, NT)]
        units = []
        for cs, j0, j1 in turns:
            units += [(0, j, c, j == j0, j == j1 - 1) for j in range(j0, j1) for c in cs]
        for g in range(1, NCH - 3):
            units += [(g, j, g + 3, j == 0, j == NT - 1) for j in range(NT)]
        NU = len(units)
        N_PAIR = NT // 2
        FIRST = next(u for u, v in enumerate(units) if v[0] == 1)

        def chunk_tiles(c):
            return min(CT, NT - c * CT)

        def bank_no(g, c, i):
            return (c % 2 * CT if g == 0 else 0) + i

        full = [(u, v[2], i) for u, v in enumerate(units) if v[4] for i in range(chunk_tiles(v[2]))]
        number = {(u, i): n + 1 for n, (u, c, i) in enumerate(full)}

        def before_bank(u, b):
            ns = [n + 1 for n, (v, c, i) in enumerate(full) if v < u and bank_no(units[v][0], c, i) == b]
            return ns[-1] if ns else 0

        last_turn = {c: u for u, c, i in full}
        first_turn = {}
        for u, c, i in full:
            first_turn.setdefault(c, u)

        need = {}
        for u, v in enumerate(units):
            need.setdefault(v[1], u)
        row_at, xs_at = {}, {}
        for j in range(NT):
            u = need[j] if j < 3 else min(4 * (j - 2) + 1, need[j])
            xs_at.setdefault(u, []).append(j)
            row_at.setdefault(max(0, u - 1), []).append(j)

        pair_at, spread = {}, {}
        for p in range(N_PAIR):
            ready = last_turn[2 * p // CT] + 2
            before = pair_at[p - 1] + 5 * spread[p - 1] if p else 0
            pair_at[p] = max(ready, before, FIRST + 1)
            spread[p] = 2 if units[min(pair_at[p], NU - 1)][2] == NCH - 1 else 1
        pair_at[N_PAIR - 1] = NU + 3
        STAGE = {"mt0": 0, "mt1": 1, "y0": 1, "elu0": 2, "y1": 3, "elu1": 4, "norm1": 5, "xt0": 5, "xt1": 7,
                 "gate": 8, "logit": 9, "rank": 10}

        def stage_at(p, name):
            return pair_at[p] + STAGE[name] * spread[p]

        REACT = RING

        def events(stages, shift):
            found = {}
            for p in range(N_PAIR):
                for name, fn in stages:
                    found.setdefault(stage_at(p, name) + shift, []).append((fn, p))
            return found

        def run(found, u):
            for fn, p in found.pop(u, ()):
                fn(p)

        def finish(found):
            for u in sorted(found):
                run(found, u)

        def dinv(t):
            return rs[:, t, 1:2]

        def wait_unit(eng, u):
            if units[u][4]:
                eng.wait_ge(bank_full, number[u, chunk_tiles(units[u][2]) - 1])
            else:
                eng.wait_ge(unit_done, sum(1 for v in units[:u + 1] if not v[4]))

        def m_tile(t):
            return m_raw[:, M_AT[t // CT], t % CT, :]

        block = ctx.enter_context(nc.Block())

        @block.sync
        def _(sp):
            def load_rows(j):
                if j >= 2:
                    sp.wait_ge(xn_done, j - 1)
                sp.dma_start(x_in[:, j % 2, :], x[j * P:(j + 1) * P, :]).then_inc(x_ld[j % 2], 16)
                for h in range(2):
                    n = 2 * j + h
                    if n >= 3:
                        sp.wait_ge(deg_done, n - 2)
                    sp.dma_start(row_in[:, n % 3, :], adj[j * P:(j + 1) * P, h * HALF:(h + 1) * HALF])\
                      .then_inc(row_ld[n % 3], 16)

            def load_weights():
                sp.wait_ge(deg_done, 2 * NT)
                sp.dma_start(w_raw[:, :, :], w.rearrange("(c p) n -> p c n", p=P)).then_inc(w_ld, 16)
                sp.dma_start(gw1_raw[:, :, :], gw1.rearrange("(c p) n -> p c n", p=P)).then_inc(w_ld, 16)

            def load_pair_x(p):
                for q in range(2):
                    if p == 0:
                        sp.wait_ge(xn_done, NT - 1 + q)
                    else:
                        sp.wait_ge(x1_st[q], 16 * p)
                        sp.wait_ge(xl_done, 2 * p - 1 + q)
                    t = 2 * p + q
                    sp.dma_start(x_in[:, q, :], x[t * P:(t + 1) * P, :]).then_inc(x_ld[q], 16)

            def load_late():
                sp.wait_ge(late_st, 16)
                sp.wait_ge(x1_done, 2 * CT)
                sp.dma_start(m_raw[:, M_AT[LATE], :, :], m_dram).then_inc(late_ld, 16)

            post = events([("y0", load_pair_x)], 4)
            post.setdefault(stage_at(3, "rank") + 1, []).append((lambda p: load_late(), None))
            post.setdefault(need[NT - 1] + 8, []).append((lambda p: load_weights(), None))
            for u, (g, j, c, first, last) in enumerate(units):
                run(post, u)
                for jj in row_at.get(u, ()):
                    load_rows(jj)
                if u >= RING:
                    sp.wait_ge(a_lo_done, u - RING + 1)
                n = chunk_tiles(c) * P
                sp.dma_start(a_raw[:, u % RING, 0:n],
                             adj_t[j * P:(j + 1) * P, c * CW:c * CW + n]).then_inc(a_ld[u % RING], 16)
                if u == 3:
                    sp.dma_start(gw2_sb[:, :, :], gw2.rearrange("(c p) n -> p c n", p=P)).then_inc(const_ld, 16)
                    sp.dma_start(gb1_sb[:, :], gb1).then_inc(const_ld, 16)
                    sp.dma_start(gb2_sb[:, :], gb2.partition_broadcast(P)).then_inc(const_ld, 16)
            finish(post)
            sp.wait_ge(phase1, 2)

            def step_loads(s, first):
                row = sp.value_load(sched[0:1, s, 0:1], min_val=0, max_val=SLOTS - S_ROWS)
                ex = sp.value_load(sched[0:1, s, 1:2], min_val=0, max_val=E - 1)
                if not first:
                    sp.wait_ge(xg_ld, 32 * s)
                sp.dma_start(list_g[:, :, :], lists[bass.ds(row, S_ROWS), :]
                             .rearrange("(p j) c -> p j c", p=P)).then_inc(lg_ld, 16)
                for m in range(4):
                    if not first:
                        sp.wait_ge(w1_lo_done, 4 * (s - 1) + m + 1)
                    sp.dma_start(w1_raw[:, :, m * 256:(m + 1) * 256],
                                 we1[bass.ds(ex, 1), :, m * 256:(m + 1) * 256]
                                 .rearrange("o (c p) n -> p (o c) n", p=P)).then_inc(w1_ld[m], 16)
                if not first:
                    sp.wait_ge(gelu_done, HC * s)
                sp.dma_start(be1_sb[:, :], be1[bass.ds(ex, 1), :, :]
                             .rearrange("o p n -> (o p) n")).then_inc(be1_ld, 16)
                for m in range(4):
                    if not first:
                        sp.wait_ge(w2_lo_done, 4 * (s - 1) + m + 1)
                    sp.dma_start(w2_raw[:, 2 * m:2 * m + 2, :],
                                 we2[bass.ds(ex, 1), m * 256:(m + 1) * 256, :]
                                 .rearrange("o (c p) n -> p (o c) n", p=P)).then_inc(w2_ld[m], 16)

            step_loads(0, True)
            with sp.Fori(1, STEPS) as s:
                step_loads(s, False)

        @block.gpsimd
        def _(pool):
            own = [0]

            def link(ins):
                own[0] += 1
                ins.then_inc(pool_own, 1)
                pool.wait_ge(pool_own, own[0])

            pool.memset(ident[:, :], 0.0).then_inc(pool_own, 1)
            pool.memset(ones[:, :], 1.0).then_inc(pool_own, 1)
            pool.memset(ones_bf[:, :], 1.0).then_inc(pool_own, 1)
            pool.memset(ln_add[:, 0:1], EPS).then_inc(pool_own, 1)
            pool.memset(ln_add[:, 1:2], 1.0).then_inc(pool_own, 1)
            pool.memset(ln_pow[:, :], -0.5).then_inc(pool_own, 1)
            pool.memset(zrow[:, :, :], 0.0).then_inc(pool_own, 1)
            own[0] = 7
            pool.wait_ge(pool_own, own[0])
            link(pool.affine_select(out=ident[:, :], in_=ident[:, :], compare_op=ALU.not_equal, fill=1.0,
                                    base=0, pattern=[[-1, P]], channel_multiplier=1))
            link(pool.affine_select(out=upper[:, :], in_=ones_bf[:, :], compare_op=ALU.is_gt, fill=0.0,
                                    base=0, pattern=[[1, P]], channel_multiplier=-1))
            link(pool.iota(cols8[:, :], [[1, E]], base=0, channel_multiplier=0,
                           allow_small_or_imprecise_dtypes=True))
            link(pool.iota(base0[:, :], [[CAP, E]], base=0, channel_multiplier=0,
                           allow_small_or_imprecise_dtypes=True))
            link(pool.iota(s_i[:, :], [[1, STEPS]], base=0, channel_multiplier=0,
                           allow_small_or_imprecise_dtypes=True))
            link(pool.iota(tok_id[:, :], [[P, NT]], base=0, channel_multiplier=1))
            link(pool.iota(pre[:, :, 0], [[1, PRE]], base=0, channel_multiplier=PRE))
            pool.nop().then_inc(consts, 1)
            pool.dma_start(xln[NP:ROWS, :].rearrange("(j p) n -> p j n", p=P), zrow[:, :, :]).then_inc(pre_st, 16)
            pool.dma_start(out[NP:ROWS, :].rearrange("(j p) n -> p j n", p=P), zrow[:, :, :]).then_inc(pre_st, 16)
            pool.wait_ge(pre_rdy, 1)
            pool.dma_start(lists.rearrange("(p c) k -> p c k", p=P), pre[:, :, :]).then_inc(pre_st, 16)

            def norm_scale(j):
                k = j % 2
                pool.wait_ge(mv_done, j + 1)
                pool.wait_ge(deg_done, 2 * j + 2)
                link(pool.tensor_tensor(pk[:, k, 0:1], mv[:, j, 1:2], ln_add[:, 0:1], ALU.add))
                link(pool.tensor_tensor(deg1[:, k, :], deg[:, j, 0:1], deg[:, j, 1:2], ALU.add))
                link(pool.tensor_tensor(pk[:, k, 1:2], deg1[:, k, :], ln_add[:, 1:2], ALU.add))
                link(pool.tensor_tensor(rs[:, j, :], pk[:, k, :], ln_pow[:, :], ALU.pow))
                pool.tensor_tensor(scl[:, j:j + 1], rs[:, j, 0:1], rs[:, j, 1:2], ALU.mult).then_inc(scl_done, 1)

            def add_self(c):
                for i in range(chunk_tiles(c)):
                    t = c * CT + i
                    m = m_late[:, i, :] if c == LATE else m_tile(t)
                    pool.wait_ge(bank_read, number[last_turn[c], i])
                    if first_turn[c] != last_turn[c]:
                        link(pool.tensor_tensor(m, m, xs_hi[:, t, :].bitcast(F32), ALU.add))
                    pool.tensor_tensor(m, m, xs_lo[:, t, :].bitcast(F32), ALU.add).then_inc(m_full, 1)
                if c == LATE:
                    pool.wait_ge(m_full, (LATE + 1) * CT)
                    pool.dma_start(m_dram, m_late[:, :, :]).then_inc(late_st, 16)

            def norm2(p, q):
                for t in (2 * p + q,):
                    pool.wait_ge(mv2_done, t + 1)
                    link(pool.tensor_tensor(pk2[:, q, :], mv2[:, q, 1:2], ln_add[:, 0:1], ALU.add))
                    pool.tensor_tensor(rstd2[:, q, :], pk2[:, q, :], ln_pow[:, 0:1], ALU.pow).then_inc(rstd2_done, 1)
                    pool.dma_start(out[t * P:(t + 1) * P, :], x_in[:, q, :]).then_inc(x1_st[q], 16)

            def store_rows(p, q):
                for t in (2 * p + q,):
                    pool.wait_ge(xl_done, t + 1)
                    pool.dma_start(xln[t * P:(t + 1) * P, :], x_n[:, q, :]).then_inc(xln_st[q], 16)

            def scatter_lists(p):
                pool.wait_ge(route_done, p + 1)
                if p == 0:
                    pool.wait_ge(pre_st, 48)
                for q in range(2):
                    for k in range(TOP_K):
                        pool.indirect_dma_start(
                            out=lists[:, :], out_offset=bass.IndirectOffsetOnAxis(
                                ap=slot[:, p % 2, q, k:k + 1].bitcast(U32), axis=0),
                            in_=pay[:, p % 2, q, k, :], in_offset=None).then_inc(list_st[p % 2], 16)

            for j in range(NT):
                norm_scale(j)
            work = []
            for c in range(NCH):
                work.append((last_turn[c] + REACT, 0, add_self, (c,)))
            for p in range(N_PAIR):
                work.append((stage_at(p, "elu0") + REACT, 1, norm2, (p, 0)))
                work.append((stage_at(p, "y1") + REACT, 2, store_rows, (p, 0)))
                work.append((stage_at(p, "elu1") + REACT, 1, norm2, (p, 1)))
                work.append((stage_at(p, "norm1") + REACT, 2, store_rows, (p, 1)))
                work.append((stage_at(p, "rank") + REACT, 3, scatter_lists, (p,)))
            for _, _, fn, args in sorted(work, key=lambda v: v[:2]):
                fn(*args)
            for q in range(2):
                pool.wait_ge(list_st[q], 16 * 2 * TOP_K * ((N_PAIR + 1 - q) // 2))
                pool.wait_ge(x1_st[q], 16 * N_PAIR)
                pool.wait_ge(xln_st[q], 16 * N_PAIR)
            pool.nop().then_inc(phase1, 1)
            pool.wait_ge(phase1, 2)

            def load_for_y(s):
                row = pool.value_load(sched[0:1, s, 0:1], min_val=0, max_val=SLOTS - S_ROWS)
                ex = pool.value_load(sched[0:1, s, 1:2], min_val=0, max_val=E - 1)
                pool.dma_start(list_y[:, :, :], lists[bass.ds(row, S_ROWS), :]
                               .rearrange("(p j) c -> p j c", p=P)).then_inc(ly_ld, 16)
                pool.dma_start(be2_sb[:, :], be2[bass.ds(ex, 1), :]
                               .rearrange("o n -> (o n)").partition_broadcast(P)).then_inc(be2_ld, 16)

            def gather(s, first):
                pool.wait_ge(lg_ld, 16 * s + 16)
                if not first:
                    pool.wait_ge(xe_ready, SJ * s)
                pool.sem_inc(waited, 1)
                for jj in range(SJ):
                    pool.indirect_dma_start(
                        out=x_g[:, jj, :], out_offset=None, in_=xln[:, :],
                        in_offset=bass.IndirectOffsetOnAxis(
                            ap=list_g[:, jj, 0:1].bitcast(U32), axis=0)).then_inc(xg_ld, 16)

            def add_rows(s):
                for jj in range(SJ):
                    pool.wait_ge(yw_done, SJ * s + jj + 1)
                    pool.sem_inc(waited, 1)
                    pool.indirect_dma_start(
                        out=out[:, :], out_offset=bass.IndirectOffsetOnAxis(
                            ap=list_y[:, jj, 0:1].bitcast(U32), axis=0),
                        in_=y_sb[:, jj, :], in_offset=None, compute_op=ALU.add).then_inc(y_add, 16)
                    pool.wait_ge(y_add, 16 * (SJ * s + jj + 1))

            gather(0, True)
            load_for_y(0)
            gather(1, False)
            with pool.Fori(1, STEPS - 1) as s:
                gather(s + 1, False)
                add_rows(s - 1)
                load_for_y(s)
            add_rows(STEPS - 2)
            load_for_y(STEPS - 1)
            add_rows(STEPS - 1)

        @block.scalar
        def _(act):
            def evac_mt(p, q):
                t = 2 * p + q
                act.wait_ge(mt_ready, t + 1)
                if t > 0:
                    act.wait_ge(y_ready, t)
                act.activation(mt_hi[:, :, :], bank[BY + q][:, :].rearrange("p (c n) -> p c n", c=DC),
                               ACT.Copy).then_inc(mt_hi_done, 1)

            def exp_neg(p, q):
                t = 2 * p + q
                act.wait_ge(neg_done, t + 1)
                act.activation(m_tile(t), m_tile(t), ACT.Exp).then_inc(exp_done, 1)

            def evac_xt(p, q):
                if p == 0 and q == 0:
                    act.wait_ge(late_st, 16)
                act.wait_ge(xt_ready, 2 * p + q + 1)
                act.activation(xt_hi[:, :, q * P:(q + 1) * P],
                               bank[BG][:, :].rearrange("p (c n) -> p c n", c=DC),
                               ACT.Copy).then_inc(xt_hi_done, 1)

            def relu_gate(p):
                act.wait_ge(g_ready, p + 1)
                act.wait_ge(const_ld, 48)
                for hb in range(GC):
                    act.activation(g_t[:, hb, :], bank[BG][:, hb * 256:(hb + 1) * 256], ACT.Relu,
                                   bias=gb1_sb[:, hb:hb + 1]).then_inc(g_done, 1)

            def exp_logits(p):
                act.wait_ge(lc_done, p + 1)
                act.activation(le[:, :, :], lc[:, :, :], ACT.Exp).then_inc(le_done, 1)
                act.wait_ge(pd_done, p + 1)
                act.activation(pe2[:, :], pd[:, :], ACT.Exp).then_inc(pe2_done, 1)

            post = events([("mt0", lambda p: evac_mt(p, 0)), ("mt1", lambda p: evac_mt(p, 1)),
                           ("y0", lambda p: exp_neg(p, 0)), ("y1", lambda p: exp_neg(p, 1)),
                           ("xt0", lambda p: evac_xt(p, 0)), ("xt1", lambda p: evac_xt(p, 1)),
                           ("gate", relu_gate), ("logit", exp_logits)], REACT)

            def split_weights(_):
                act.wait_ge(w_ld, 32)
                act.activation(w_hi[:, :, :], w_raw[:, :, :], ACT.Copy).then_inc(w_hi_done, 1)
                act.activation(gw1_hi[:, :, :], gw1_raw[:, :, :], ACT.Copy).then_inc(w_hi_done, 1)

            post.setdefault(FIRST - 4, []).append((split_weights, None))

            def degree(j):
                for n in (2 * j, 2 * j + 1):
                    act.wait_ge(row_ld[n % 3], 16 * (n // 3 + 1))
                    act.activation(row_in[:, n % 3, :], row_in[:, n % 3, :], ACT.Copy,
                                   accum_out=deg[:, j, n % 2:n % 2 + 1]).then_inc(deg_done, 1)

            def xs_split(j):
                act.wait_ge(xn_done, j + 1)
                act.activation(xs_hi[:, j, :], x_n[:, j % 2, :], ACT.Copy).then_inc(xs_hi_done, 1)

            for u, (g, j, c, first, last) in enumerate(units):
                run(post, u)
                for jj in row_at.get(u, ()):
                    degree(jj)
                for jj in xs_at.get(u, ()):
                    xs_split(jj)
                n = chunk_tiles(c) * P
                act.wait_ge(a_ld[u % RING], 16 * (u // RING + 1))
                if u >= RING:
                    wait_unit(act, u - RING)
                act.activation(a_hi[:, u % RING, 0:n], a_raw[:, u % RING, 0:n], ACT.Copy).then_inc(a_hi_done, 1)
            finish(post)
            act.wait_ge(phase1, 2)

            def w1_split(s, m, first):
                act.wait_ge(w1_ld[m], 16 * s + 16)
                if not first:
                    act.wait_ge(h_ready, HC * (s - 1) + 2 * m + 2)
                act.activation(w1_hi[:, :, m * 256:(m + 1) * 256], w1_raw[:, :, m * 256:(m + 1) * 256],
                               ACT.Copy).then_inc(w1_hi_done, 1)

            def w2_split(s, m, first):
                act.wait_ge(w2_ld[m], 16 * s + 16)
                if not first:
                    if m < 3:
                        act.wait_ge(w2_used, 3 * (s - 1) + m + 1)
                    else:
                        act.wait_ge(ye_ready, SJ * s)
                act.activation(w2_hi[:, 2 * m:2 * m + 2, :], w2_raw[:, 2 * m:2 * m + 2, :],
                               ACT.Copy).then_inc(w2_hi_done, 1)

            def xe_split(s):
                for jj in range(SJ):
                    act.wait_ge(xe_ready, SJ * s + jj + 1)
                    act.activation(xe_hi[:, :, jj * P:(jj + 1) * P],
                                   bank[jj][:, :].rearrange("p (c n) -> p c n", c=DC),
                                   ACT.Copy).then_inc(xe_hi_done, 1)

            def step(s, nxt):
                act.wait_ge(be1_ld, 16 * s + 16)
                for m in range(4):
                    hb = bank[2 + m]
                    act.wait_ge(h_ready, HC * s + 2 * m + 2)
                    for k in range(2):
                        act.activation(hb[:, k * 256:(k + 1) * 256], hb[:, k * 256:(k + 1) * 256], ACT.Gelu,
                                       bias=be1_sb[:, 2 * m + k:2 * m + k + 1]).then_inc(gelu_done, 1)
                    act.wait_ge(gelu_done, HC * s + 2 * m + 2)
                    act.activation(h_hi[:, 2 * m:2 * m + 2, :], hb[:, :].rearrange("p (k n) -> p k n", k=2),
                                   ACT.Copy).then_inc(h_hi_done, 1)
                    if nxt:
                        w1_split(s + 1, m, False)
                if nxt:
                    xe_split(s + 1)
                    for m in range(4):
                        w2_split(s + 1, m, False)

            for m in range(4):
                w1_split(0, m, True)
            xe_split(0)
            for m in range(4):
                w2_split(0, m, True)
            step(0, True)
            with act.Fori(1, STEPS - 1) as s:
                step(s, True)
            step(STEPS - 1, False)

        @block.vector
        def _(dve):
            own = [0]

            def link(ins):
                own[0] += 1
                ins.then_inc(dve_own, 1)
                dve.wait_ge(dve_own, own[0])

            dve.wait_ge(consts, 1)
            link(dve.tensor_scalar(pre[:, :, 0], pre[:, :, 0], S_ROWS - 1, None, ALU.bitwise_and))
            link(dve.tensor_scalar(pre[:, :, 0], pre[:, :, 0], float(DUMMY), None, ALU.add))
            link(dve.memset(pre[:, :, 1], 0))
            dve.nop().then_inc(pre_rdy, 1)
            link(dve.tensor_copy(base[:, :], base0[:, :]))

            def stats(j):
                dve.wait_ge(x_ld[j % 2], 16 * (j // 2 + 1))
                link(dve.bn_stats(stat6[:, j % 2, :], x_in[:, j % 2, :]))
                dve.bn_aggr(mv[:, j, :], stat6[:, j % 2, :]).then_inc(mv_done, 1)

            def xs_make(j):
                dve.wait_ge(scl_done, j + 1)
                dve.wait_ge(mv_done, j + 1)
                if j >= 2:
                    dve.wait_ge(xs_lo_done, j - 1)
                dve.tensor_scalar(x_n[:, j % 2, :], x_in[:, j % 2, :], mv[:, j, 0:1], scl[:, j:j + 1],
                                  ALU.subtract, ALU.mult).then_inc(xn_done, 1)

            def xs_rest(j):
                dve.wait_ge(xs_hi_done, j + 1)
                dve.tensor_tensor(xs_lo[:, j, :], x_n[:, j % 2, :], xs_hi[:, j, :].bitcast(F32),
                                  ALU.subtract).then_inc(xs_lo_done, 1)

            def read_banks(u):
                g, _, c, _, _ = units[u]
                for i in range(chunk_tiles(c)):
                    t = c * CT + i
                    m = m_late[:, i, :] if c == LATE else m_tile(t)
                    dve.wait_ge(bank_full, number[u, i])
                    if c < 2 and i == 0 and u == first_turn[c]:
                        dve.wait_ge(pre_st, 48)
                    src = bank[bank_no(g, c, i)][:, :]
                    if first_turn[c] == last_turn[c]:
                        dve.tensor_tensor(m, src, xs_hi[:, t, :].bitcast(F32), ALU.add).then_inc(bank_read, 1)
                    elif u == first_turn[c]:
                        dve.tensor_copy(m, src).then_inc(bank_read, 1)
                    else:
                        dve.tensor_tensor(m, m, src, ALU.add).then_inc(bank_read, 1)

            def mt_rest(p, q):
                dve.wait_ge(mt_hi_done, 2 * p + q + 1)
                dve.tensor_tensor(mt_lo[:, :, :], bank[BY + q][:, :].rearrange("p (c n) -> p c n", c=DC),
                                  mt_hi[:, :, :].bitcast(F32), ALU.subtract).then_inc(mt_lo_done, 1)

            def neg_part(p, q):
                t = 2 * p + q
                dve.wait_ge(y_ready, t + 1)
                dve.tensor_scalar(m_tile(t), bank[BY + q][:, :], dinv(t), 0.0,
                                  ALU.mult, ALU.min).then_inc(neg_done, 1)

            def elu(p, q):
                t = 2 * p + q
                dve.wait_ge(exp_done, t + 1)
                link(dve.tensor_scalar(m_tile(t), m_tile(t), -1.0, None, ALU.add))
                link(dve.scalar_tensor_tensor(m_tile(t), bank[BY + q][:, :], dinv(t), m_tile(t),
                                              ALU.mult, ALU.max))
                dve.wait_ge(x_ld[q], 16 * (NT // 2 + p + 1))
                dve.tensor_tensor(x_in[:, q, :], m_tile(t), x_in[:, q, :], ALU.add).then_inc(x1_done, 1)
                dve.wait_ge(x1_done, t + 1)
                link(dve.bn_stats(stat6[:, q, :], x_in[:, q, :]))
                dve.bn_aggr(mv2[:, q, :], stat6[:, q, :]).then_inc(mv2_done, 1)

            def norm(p, q):
                t = 2 * p + q
                dve.wait_ge(rstd2_done, t + 1)
                dve.wait_ge(mv2_done, t + 1)
                if p > 0:
                    dve.wait_ge(xln_st[q], 16 * p)
                dve.tensor_scalar(x_n[:, q, :], x_in[:, q, :], mv2[:, q, 0:1], rstd2[:, q, :],
                                  ALU.subtract, ALU.mult).then_inc(xl_done, 1)

            def xt_rest(p, q):
                dve.wait_ge(xt_hi_done, 2 * p + q + 1)
                dve.tensor_tensor(xt_lo[:, :, q * P:(q + 1) * P],
                                  bank[BG][:, :].rearrange("p (c n) -> p c n", c=DC),
                                  xt_hi[:, :, q * P:(q + 1) * P].bitcast(F32),
                                  ALU.subtract).then_inc(xt_lo_done, 1)

            def experts(p):
                dve.wait_ge(l_ready, p + 1)
                dve.wait_ge(const_ld, 48)
                link(dve.tensor_tensor(lg[:, :, :], bank[BS][:, L_AT:L_AT + 2 * E].rearrange("p (q e) -> p q e", q=2),
                                       gb2_sb[:, :].unsqueeze(1).to_broadcast([P, 2, E]), ALU.add))
                link(dve.tensor_reduce(lmax[:, :], lg[:, :, :], AX.X, ALU.max))
                dve.tensor_tensor(lc[:, :, :], lg[:, :, :], lmax[:, :].unsqueeze(2).to_broadcast([P, 2, E]),
                                  ALU.subtract).then_inc(lc_done, 1)
                dve.wait_ge(le_done, p + 1)
                link(dve.tensor_reduce(lsum[:, :], le[:, :, :], AX.X, ALU.add))
                link(dve.reciprocal(lrec[:, :], lsum[:, :]))
                link(dve.tensor_tensor(prob[:, :, :], le[:, :, :], lrec[:, :].unsqueeze(2).to_broadcast([P, 2, E]),
                                       ALU.mult))
                for q in range(2):
                    link(dve.max(top[:, q, :], prob[:, q, :]))
                dve.tensor_tensor(pd[:, :], top[:, :, 1], top[:, :, 0], ALU.subtract).then_inc(pd_done, 1)
                for q in range(2):
                    link(dve.max_index(topi[:, q, :], top[:, q, :], prob[:, q, :]))
                link(dve.tensor_copy(topf[:, :, :], topi[:, :, :]))
                for q in range(2):
                    for k in range(TOP_K):
                        link(dve.tensor_scalar(hot[:, q, k, :], cols8[:, :], topf[:, q, k:k + 1], None, ALU.is_equal))
                dve.tensor_tensor(mask[:, :, :], hot[:, :, 0, :], hot[:, :, 1, :], ALU.add).then_inc(mask_done, 1)
                dve.wait_ge(pe2_done, p + 1)
                link(dve.tensor_scalar(pden[:, :], pe2[:, :], 1.0, None, ALU.add))
                link(dve.reciprocal(wts[:, :, 0], pden[:, :]))
                link(dve.tensor_tensor(wts[:, :, 1], wts[:, :, 0], pe2[:, :], ALU.mult))

            def slots(p):
                b = p % 2
                dve.wait_ge(r_ready, p + 1)
                link(dve.tensor_tensor(rb[:, :, :], bank[BS][:, R_AT:R_AT + 2 * E].rearrange("p (q e) -> p q e", q=2),
                                       base[:, :].unsqueeze(1).to_broadcast([P, 2, E]), ALU.add))
                link(dve.tensor_tensor(pick[:, :, :, :], hot[:, :, :, :],
                                       rb[:, :, :].unsqueeze(2).to_broadcast([P, 2, TOP_K, E]), ALU.mult))
                link(dve.tensor_reduce(slotf[:, :, :], pick[:, :, :, :], AX.X, ALU.add))
                if p >= 2:
                    dve.wait_ge(list_st[b], 16 * 2 * TOP_K * (p // 2))
                link(dve.tensor_copy(slot[:, b, :, :], slotf[:, :, :]))
                link(dve.tensor_copy(pay[:, b, :, :, 0],
                                     tok_id[:, 2 * p:2 * p + 2].unsqueeze(2).to_broadcast([P, 2, TOP_K])))
                link(dve.tensor_copy(pay[:, b, :, :, 1].bitcast(F32), wts[:, :, :]))
                dve.tensor_tensor(base[:, :], base[:, :], bank[BS][:, C_AT:C_AT + E], ALU.add).then_inc(route_done, 1)
                dve.wait_ge(route_done, p + 1)

            def rest_weights(_):
                dve.wait_ge(w_hi_done, 2)
                dve.tensor_tensor(w_lo[:, :, :], w_raw[:, :, :], w_hi[:, :, :].bitcast(F32),
                                  ALU.subtract).then_inc(w_lo_done, 1)
                dve.tensor_tensor(gw1_lo[:, :, :], gw1_raw[:, :, :], gw1_hi[:, :, :].bitcast(F32),
                                  ALU.subtract).then_inc(w_lo_done, 1)

            post = events([("mt0", lambda p: mt_rest(p, 0)), ("y0", lambda p: neg_part(p, 0)),
                           ("mt1", lambda p: mt_rest(p, 1)), ("elu0", lambda p: elu(p, 0)),
                           ("y1", lambda p: neg_part(p, 1)), ("y1", lambda p: norm(p, 0)),
                           ("xt0", lambda p: xt_rest(p, 0)), ("elu1", lambda p: elu(p, 1)),
                           ("norm1", lambda p: norm(p, 1)), ("xt1", lambda p: xt_rest(p, 1)),
                           ("logit", experts), ("rank", slots)], REACT)
            for u in sorted({v for v, _, _ in full}):
                post.setdefault(u + RING - 1, []).append((read_banks, u))
            post.setdefault(FIRST - 4, []).append((rest_weights, None))
            for u, (g, j, c, first, last) in enumerate(units):
                run(post, u)
                for jj in row_at.get(u, ()):
                    stats(jj)
                for jj in xs_at.get(u, ()):
                    xs_make(jj)
                    xs_rest(jj)
                n = chunk_tiles(c) * P
                dve.wait_ge(a_hi_done, u + 1)
                dve.tensor_tensor(a_lo[:, u % RING, 0:n], a_raw[:, u % RING, 0:n],
                                  a_hi[:, u % RING, 0:n].bitcast(F32), ALU.subtract).then_inc(a_lo_done, 1)
            finish(post)

            link(dve.tensor_tensor(cnt[:, :], base[:, :], base0[:, :], ALU.subtract))
            link(dve.tensor_scalar(tiles_i[:, :], cnt[:, :], float(S_ROWS - 1), None, ALU.add))
            link(dve.tensor_scalar(tiles_i[:, :], tiles_i[:, :], S_ROWS.bit_length() - 1, None,
                                   ALU.logical_shift_right))
            link(dve.tensor_copy(tiles_f[:, :], tiles_i[:, :]))
            link(dve.tensor_copy(cum[:, 0, :], tiles_f[:, :]))
            for n, d in enumerate((1, 2, 4)):
                link(dve.tensor_copy(cum[:, n + 1, 0:d], cum[:, n, 0:d]))
                link(dve.tensor_tensor(cum[:, n + 1, d:E], cum[:, n, d:E], cum[:, n, 0:E - d], ALU.add))
            link(dve.tensor_tensor(past[:, :, :], cum[:, 3, :].unsqueeze(1).to_broadcast([P, STEPS, E]),
                                   s_i[:, :].unsqueeze(2).to_broadcast([P, STEPS, E]), ALU.is_le))
            link(dve.tensor_tensor(past_t[:, :, :], past[:, :, :],
                                   tiles_f[:, :].unsqueeze(1).to_broadcast([P, STEPS, E]), ALU.mult))
            link(dve.tensor_reduce(s_e[:, :], past[:, :, :], AX.X, ALU.add))
            link(dve.tensor_reduce(s_t[:, :], past_t[:, :, :], AX.X, ALU.add))
            link(dve.tensor_tensor(s_t[:, :], s_i[:, :], s_t[:, :], ALU.subtract))
            link(dve.tensor_scalar(s_t[:, :], s_t[:, :], float(S_ROWS), None, ALU.mult))
            link(dve.tensor_scalar(s_r[:, :, 1], s_e[:, :], float(E - 1), None, ALU.min))
            link(dve.tensor_scalar(s_r[:, :, 0], s_e[:, :], float(CAP), None, ALU.mult))
            link(dve.tensor_tensor(s_r[:, :, 0], s_r[:, :, 0], s_t[:, :], ALU.add))
            dve.tensor_copy(sched[:, :, :], s_r[:, :, :]).then_inc(phase1, 1)
            dve.wait_ge(phase1, 2)

            def w1_rest(s, m):
                dve.wait_ge(w1_hi_done, 4 * s + m + 1)
                dve.tensor_tensor(w1_lo[:, :, m * 256:(m + 1) * 256], w1_raw[:, :, m * 256:(m + 1) * 256],
                                  w1_hi[:, :, m * 256:(m + 1) * 256].bitcast(F32),
                                  ALU.subtract).then_inc(w1_lo_done, 1)

            def w2_rest(s, m):
                dve.wait_ge(w2_hi_done, 4 * s + m + 1)
                dve.tensor_tensor(w2_lo[:, 2 * m:2 * m + 2, :], w2_raw[:, 2 * m:2 * m + 2, :],
                                  w2_hi[:, 2 * m:2 * m + 2, :].bitcast(F32),
                                  ALU.subtract).then_inc(w2_lo_done, 1)

            def xe_rest(s):
                for jj in range(SJ):
                    dve.wait_ge(xe_hi_done, SJ * s + jj + 1)
                    dve.tensor_tensor(xe_lo[:, :, jj * P:(jj + 1) * P],
                                      bank[jj][:, :].rearrange("p (c n) -> p c n", c=DC),
                                      xe_hi[:, :, jj * P:(jj + 1) * P].bitcast(F32),
                                      ALU.subtract).then_inc(xe_lo_done, 1)

            def weigh(s, first):
                dve.wait_ge(be2_ld, 16 * s + 16)
                dve.wait_ge(ly_ld, 16 * s + 16)
                for jj in range(SJ):
                    dve.wait_ge(ye_ready, SJ * s + jj + 1)
                    if not first:
                        dve.wait_ge(y_add, 16 * (SJ * (s - 1) + jj + 1))
                    dve.tensor_tensor(y_sb[:, jj, :], bank[6 + jj][:, :], be2_sb[:, :], ALU.add).then_inc(yb_done, 1)
                    dve.wait_ge(yb_done, SJ * s + jj + 1)
                    dve.tensor_scalar(y_sb[:, jj, :], y_sb[:, jj, :], list_y[:, jj, 1:2].bitcast(F32), None,
                                      ALU.mult).then_inc(yw_done, 1)

            def step(s, nxt, earlier):
                for m in range(4):
                    dve.wait_ge(h_hi_done, 4 * s + m + 1)
                    dve.tensor_tensor(h_lo[:, 2 * m:2 * m + 2, :], bank[2 + m][:, :].rearrange("p (k n) -> p k n", k=2),
                                      h_hi[:, 2 * m:2 * m + 2, :].bitcast(F32), ALU.subtract).then_inc(h_lo_done, 1)
                    if m == 0 and earlier > 0:
                        weigh(s - 1, earlier == 1)
                    if nxt:
                        w1_rest(s + 1, m)
                if nxt:
                    xe_rest(s + 1)
                    for m in range(4):
                        w2_rest(s + 1, m)

            for m in range(4):
                w1_rest(0, m)
            xe_rest(0)
            for m in range(4):
                w2_rest(0, m)
            step(0, True, 0)
            step(1, True, 1)
            with dve.Fori(2, STEPS - 1) as s:
                step(s, True, 2)
            step(STEPS - 1, False, 2)
            weigh(STEPS - 1, False)

        @block.tensor
        def _(pe):
            def three(dst, a_h, a_l, b_h, b_l, start, stop):
                pe.matmul(dst, a_h, b_h, start=start, stop=False)
                pe.matmul(dst, a_h, b_l, start=False, stop=False)
                return pe.matmul(dst, a_l, b_h, start=False, stop=stop)

            def transpose_m(p, q):
                t = 2 * p + q
                if t // CT == LATE:
                    pe.wait_ge(late_ld, 16)
                else:
                    pe.wait_ge(m_full, t + 1)
                if p == 0:
                    pe.wait_ge(bank_read, before_bank(NU, BY + 3))
                else:
                    pe.wait_ge(x1_done, t - 1)
                for d in range(DC):
                    last = pe.transpose(bank[BY + q][:, d * P:(d + 1) * P],
                                        m_tile(t)[:, d * P:(d + 1) * P], ident[:, :])
                last.then_inc(mt_ready, 1)

            def project(p, q):
                t = 2 * p + q
                pe.wait_ge(mt_lo_done, t + 1)
                pe.wait_ge(w_lo_done, 2)
                for d in range(DC):
                    last = three(bank[BY + q][:, :], mt_hi[:, d, :], mt_lo[:, d, :],
                                 w_hi[:, d, :], w_lo[:, d, :], d == 0, d == DC - 1)
                last.then_inc(y_ready, 1)

            def transpose_x(p, q):
                t = 2 * p + q
                pe.wait_ge(xl_done, t + 1)
                pe.wait_ge(xt_lo_done, t)
                if p > 0:
                    pe.wait_ge(g_done, GC * p)
                for d in range(DC):
                    last = pe.transpose(bank[BG][:, d * P:(d + 1) * P], x_n[:, q, d * P:(d + 1) * P],
                                        ident[:, :])
                last.then_inc(xt_ready, 1)

            def gate(p):
                pe.wait_ge(xt_lo_done, 2 * p + 2)
                for hb in range(GC):
                    for d in range(DC):
                        last = three(bank[BG][:, hb * 256:(hb + 1) * 256],
                                     gw1_hi[:, d, hb * P:(hb + 1) * P], gw1_lo[:, d, hb * P:(hb + 1) * P],
                                     xt_hi[:, d, :], xt_lo[:, d, :], d == 0, d == DC - 1)
                last.then_inc(g_ready, 1)

            def logits(p):
                pe.wait_ge(g_done, GC * (p + 1))
                pe.wait_ge(const_ld, 48)
                if p > 0:
                    pe.wait_ge(route_done, p)
                for q in range(2):
                    for hb in range(GC):
                        last = pe.matmul(bank[BS][:, L_AT + q * E:L_AT + (q + 1) * E], g_t[:, hb, q * P:(q + 1) * P],
                                         gw2_sb[:, hb, :], start=hb == 0, stop=hb == GC - 1)
                last.then_inc(l_ready, 1)

            def ranks(p):
                pe.wait_ge(mask_done, p + 1)
                r = bank[BS]
                pe.matmul(r[:, R_AT:R_AT + E], upper[:, :], mask[:, 0, :], start=True, stop=True)
                pe.matmul(r[:, R_AT + E:R_AT + 2 * E], upper[:, :], mask[:, 1, :], start=True, stop=False)
                pe.matmul(r[:, R_AT + E:R_AT + 2 * E], ones_bf[:, :], mask[:, 0, :], start=False, stop=True)
                pe.matmul(r[:, C_AT:C_AT + E], ones_bf[:, :], mask[:, 0, :], start=True, stop=False)
                pe.matmul(r[:, C_AT:C_AT + E], ones_bf[:, :], mask[:, 1, :], start=False,
                          stop=True).then_inc(r_ready, 1)

            post = events([("mt0", lambda p: transpose_m(p, 0)), ("mt1", lambda p: transpose_m(p, 1)),
                           ("y0", lambda p: project(p, 0)), ("y1", lambda p: project(p, 1)),
                           ("xt0", lambda p: transpose_x(p, 0)), ("xt1", lambda p: transpose_x(p, 1)), ("gate", gate), ("logit", logits), ("rank", ranks)], 0)
            pe.wait_ge(consts, 1)
            for u, (g, j, c, first, closes) in enumerate(units):
                pe.wait_ge(xs_lo_done, j + 1)
                pe.wait_ge(a_lo_done, u + 1)
                k = u % RING
                for i in range(chunk_tiles(c)):
                    b = bank_no(g, c, i)
                    if first and before_bank(u, b):
                        pe.wait_ge(bank_read, before_bank(u, b))
                    last = three(bank[b][:, :], a_hi[:, k, i * P:(i + 1) * P], a_lo[:, k, i * P:(i + 1) * P],
                                 xs_hi[:, j, :], xs_lo[:, j, :], first, closes)
                    if closes:
                        last.then_inc(bank_full, 1)
                if not closes:
                    last.then_inc(unit_done, 1)
                run(post, u)
            finish(post)
            pe.wait_ge(phase1, 2)

            def transpose_xe(s, first):
                if not first:
                    pe.wait_ge(xe_lo_done, SJ * s)
                for jj in range(SJ):
                    pe.wait_ge(xg_ld, 16 * (SJ * s + SJ))
                    for d in range(DC):
                        last = pe.transpose(bank[jj][:, d * P:(d + 1) * P], x_g[:, jj, d * P:(d + 1) * P],
                                            ident[:, :])
                    last.then_inc(xe_ready, 1)

            def step(s, nxt, first):
                pe.wait_ge(xe_lo_done, SJ * s + SJ)
                for k in range(HC):
                    if k % 2 == 0:
                        pe.wait_ge(w1_lo_done, 4 * s + k // 2 + 1)
                        if not first:
                            pe.wait_ge(h_lo_done, 4 * (s - 1) + k // 2 + 1)
                    for d in range(DC):
                        last = three(bank[2 + k // 2][:, k % 2 * 256:k % 2 * 256 + 256],
                                     w1_hi[:, d, k * P:(k + 1) * P], w1_lo[:, d, k * P:(k + 1) * P],
                                     xe_hi[:, d, :], xe_lo[:, d, :], d == 0, d == DC - 1)
                    last.then_inc(h_ready, 1)
                if nxt:
                    transpose_xe(s + 1, False)
                if not first:
                    pe.wait_ge(yw_done, SJ * s)
                for k in range(HC):
                    if k % 2 == 0:
                        pe.wait_ge(w2_lo_done, 4 * s + k // 2 + 1)
                        pe.wait_ge(h_lo_done, 4 * s + k // 2 + 1)
                    for jj in range(SJ):
                        last = three(bank[6 + jj][:, :], h_hi[:, k, jj * P:(jj + 1) * P], h_lo[:, k, jj * P:(jj + 1) * P],
                                     w2_hi[:, k, :], w2_lo[:, k, :], k == 0, k == HC - 1)
                        if k == HC - 1:
                            last.then_inc(ye_ready, 1)
                        elif k % 2 and jj == SJ - 1:
                            last.then_inc(w2_used, 1)

            transpose_xe(0, True)
            step(0, True, True)
            with pe.Fori(1, STEPS - 1) as s:
                step(s, True, False)
            step(STEPS - 1, False, False)


def kernel(x, adj, L0_gnn_w, L0_ffn_gw1, L0_ffn_gb1, L0_ffn_gw2, L0_ffn_gb2, L0_ffn_we1, L0_ffn_be1,
           L0_ffn_we2, L0_ffn_be2):
    import numpy as np
    import concourse.bacc as bacc
    from concourse import mybir as mb
    from concourse.bass_utils import run_bass_kernel_spmd

    x_p = np.zeros((NP, D), np.float32)
    x_p[:N_TOK] = np.asarray(x)
    a_p = np.zeros((NP, NP), np.float32)
    a_p[:N_TOK, :N_TOK] = np.asarray(adj)
    arrays = {
        "x_in": x_p,
        "adj_in": a_p,
        "adj_t_in": np.ascontiguousarray(a_p.T),
        "w_in": np.ascontiguousarray(L0_gnn_w),
        "gw1_in": np.ascontiguousarray(L0_ffn_gw1),
        "gb1_in": np.ascontiguousarray(np.asarray(L0_ffn_gb1).reshape(GC, P).T),
        "gw2_in": np.ascontiguousarray(L0_ffn_gw2),
        "gb2_in": np.ascontiguousarray(L0_ffn_gb2),
        "we1_in": np.ascontiguousarray(L0_ffn_we1),
        "be1_in": np.ascontiguousarray(np.asarray(L0_ffn_be1).reshape(E, HC, P).transpose(0, 2, 1)),
        "we2_in": np.ascontiguousarray(L0_ffn_we2),
        "be2_in": np.ascontiguousarray(L0_ffn_be2),
    }
    nc = bacc.Bacc("TRN2", target_bir_lowering=False, num_devices=1)
    args = [nc.dram_tensor(n, a.shape, mb.dt.from_np(a.dtype), kind="ExternalInput").ap() for n, a in arrays.items()]
    args.append(nc.dram_tensor("out_rows", (ROWS, D), F32, kind="ExternalOutput").ap())
    build(nc, *args)
    r = run_bass_kernel_spmd(nc, [arrays], core_ids=[0])
    return r.results[0]["out_rows"][:N_TOK]
```

```python
import concourse.bass as bass
from concourse import mybir
from contextlib import ExitStack

F32 = mybir.dt.float32
F32R = mybir.dt.float32r
BF16 = mybir.dt.bfloat16
I32 = mybir.dt.int32
U32 = mybir.dt.uint32
ALU = mybir.AluOpType
ACT = mybir.ActivationFunctionType
AX = mybir.AxisListType

P = 128
N_TOK = 3327
NT = -(-N_TOK // P)
NP = NT * P
D = 512
DC = D // P
GH = 256
GC = GH // P
E = 8
H = 1024
HC = H // P
TOP_K = 2
EPS = 1e-5

S_ROWS = 256
SJ = S_ROWS // P
CAP = -(-NP // S_ROWS) * S_ROWS
STEPS = (TOP_K * NP + E * (S_ROWS - 1)) // S_ROWS
EARLY = 2
DUMMY = NP
ROWS = NP + S_ROWS
SLOTS = (E + 1) * CAP

assert TOP_K * (NP - 2 * P) >= E * EARLY * S_ROWS

CW = 512
CT = CW // P
NCH = -(-NP // CW)
RING = 4
X_RING = 3


def build(nc, x, adj, adj_t, w, gw1, gb1, gw2, gb2, we1, be1, we2, be2, out):
    ctx = ExitStack()
    with ctx:
        arena = [-(-nc.sbuf_base // 32) * 32]

        def at(name, shape, dt):
            n = 1
            for k in shape[1:]:
                n *= k
            size = -(-n * (2 if dt == BF16 else 4) // 32) * 32
            t = nc.alloc_sbuf_tensor_at(name, shape, dt, offset=arena[0])
            arena[0] += size
            return t

        def sem(name):
            return ctx.enter_context(nc.semaphore(name))

        ident = at("ident", [P, P], F32)
        ones = at("ones", [P, P], F32)
        upper = at("upper", [P, P], BF16)
        ones_bf = at("ones_bf", [P, P], BF16)
        ln_add = at("ln_add", [P, 2], F32)
        ln_pow = at("ln_pow", [P, 2], F32)
        sched = at("sched", [P, STEPS, 3], I32)
        early = at("early", [P, 2], I32)
        cols8 = at("cols8", [P, E], F32)
        tok_id = at("tok_id", [P, NT], I32)
        base0 = at("base0", [P, E], F32)
        base = at("base", [P, E], F32)
        common_end = arena[0]

        zs_hi = at("zs_hi", [P, NT, D], F32R)
        zs_lo = at("zs_lo", [P, NT, D], F32R)
        a_raw = at("a_raw", [P, RING, CW], F32)
        a_hi = at("a_hi", [P, RING, CW], F32R)
        a_lo = at("a_lo", [P, RING, CW], F32R)
        x_at = arena[0]
        x_in = at("x_in", [P, X_RING, D], F32)
        x_n = at("x_n", [P, 2, D], F32)
        e_neg = at("e_neg", [P, 2, D], F32)
        stat6 = at("stat6", [P, 2, 6], F32)
        mv = at("mv", [P, NT, 2], F32)
        pk = at("pk", [P, 2, 2], F32)
        rs = at("rs", [P, NT, 2], F32)
        deg = at("deg", [P, NT, 2], F32)
        deg1 = at("deg1", [P, 2, 1], F32)
        gb1_sb = at("gb1_sb", [P, GC], F32)
        gw2_sb = at("gw2_sb", [P, GC, E], F32)
        gb2_sb = at("gb2_sb", [P, E], F32)
        mv2 = at("mv2", [P, 2, 2], F32)
        pk2 = at("pk2", [P, 2, 1], F32)
        rstd2 = at("rstd2", [P, 2, 1], F32)
        lg = at("lg", [P, 2, E], F32)
        lmax = at("lmax", [P, 2], F32)
        lc = at("lc", [P, 2, E], F32)
        le = at("le", [P, 2, E], F32)
        lsum = at("lsum", [P, 2], F32)
        lrec = at("lrec", [P, 2], F32)
        prob = at("prob", [P, 2, E], F32)
        top = at("top", [P, 2, 8], F32)
        topi = at("topi", [P, 2, 8], U32)
        topf = at("topf", [P, 2, 8], F32)
        hot = at("hot", [P, 2, TOP_K, E], F32)
        mask = at("mask", [P, 2, E], BF16)
        pd = at("pd", [P, 2], F32)
        pe2 = at("pe2", [P, 2], F32)
        pden = at("pden", [P, 2], F32)
        wts = at("wts", [P, 2, TOP_K], F32)
        rb = at("rb", [P, 2, E], F32)
        pick = at("pick", [P, 2, TOP_K, E], F32)
        slotf = at("slotf", [P, 2, TOP_K], F32)
        slot = at("slot", [P, 2, 2, TOP_K], I32)
        pay = at("pay", [P, 2, 2, TOP_K, 2], I32)
        cnt = at("cnt", [P, E], F32)
        tiles_i = at("tiles_i", [P, E], I32)
        tiles_f = at("tiles_f", [P, E], F32)
        cum = at("cum", [P, 4, E], F32)
        most = at("most", [P, 8], F32)
        most_i = at("most_i", [P, 8], U32)
        e_star = at("e_star", [P, 2], F32)
        e_hot = at("e_hot", [P, E], F32)
        e_row = at("e_row", [P, STEPS], F32)
        s_i = at("s_i", [P, STEPS], F32)
        past = at("past", [P, STEPS, E], F32)
        past_t = at("past_t", [P, STEPS, E], F32)
        s_e = at("s_e", [P, STEPS], F32)
        s_t = at("s_t", [P, STEPS], F32)
        s_r = at("s_r", [P, STEPS, 3], F32)
        HALF = NP // 2
        rows_at = arena[0]
        row_in = at("row_in", [P, 3, HALF], F32)
        rows_end = arena[0]

        def over(name, shape, dt, place):
            return nc.alloc_sbuf_tensor_at(name, shape, dt, offset=place)

        nt_at = arena[0]
        nt_hi = at("nt_hi", [P, 2, DC, P], F32R)
        nt_lo = at("nt_lo", [P, 2, DC, P], F32R)
        w_at = arena[0]
        w_raw = over("w_raw", [P, DC, D], F32, w_at)
        w_lo = at("w_lo", [P, DC, D], F32R)
        w_hi = at("w_hi", [P, DC, D], F32R)
        phase1_end = arena[0]
        Y_RING = 6
        y_raw = over("y_raw", [P, Y_RING, D], F32, w_at)
        arena[0] = rows_at
        gw1_raw = over("gw1_raw", [P, DC, GH], F32, arena[0])
        gw1_lo = at("gw1_lo", [P, DC, GH], F32R)
        gw1_hi = at("gw1_hi", [P, DC, GH], F32R)
        xt_hi = at("xt_hi", [P, DC, 2 * P], F32R)
        xt_lo = at("xt_lo", [P, DC, 2 * P], F32R)
        g_t = at("g_t", [P, GC, 2 * P], F32)
        arena[0] = phase1_end

        PRE = SLOTS // P
        pre = over("pre", [P, PRE, 2], I32, common_end + (NT - 1) * D * 4)
        zrow = over("zrow", [P, SJ, D], F32, common_end + (2 * NT - SJ) * D * 4)

        arena[0] = common_end
        w1_raw = at("w1_raw", [P, DC, H], F32)
        w2_raw = at("w2_raw", [P, HC, D], F32)
        w1_hi = at("w1_hi", [P, DC, H], F32R)
        w1_lo = at("w1_lo", [P, DC, H], F32R)
        w2_hi = at("w2_hi", [P, HC, D], F32R)
        w2_lo = at("w2_lo", [P, HC, D], F32R)
        xe_hi = at("xe_hi", [P, DC, S_ROWS], F32R)
        xe_lo = at("xe_lo", [P, DC, S_ROWS], F32R)
        h_hi = at("h_hi", [P, HC, S_ROWS], F32R)
        h_lo = at("h_lo", [P, HC, S_ROWS], F32R)
        y_sb = at("y_sb", [P, SJ, D], F32)
        assert arena[0] <= x_at
        arena[0] = nt_at
        x_g = at("x_g", [P, SJ, D], F32)
        be1_sb = at("be1_sb", [P, HC], F32)
        be2_sb = at("be2_sb", [P, D], F32)
        list_e = at("list_e", [P, EARLY, SJ, 2], I32)
        list_g = at("list_g", [P, SJ, 2], I32)
        list_y = at("list_y", [P, SJ, 2], I32)
        assert arena[0] <= w_at

        bank = [ctx.enter_context(nc.psum_tensor(f"bank{b}", [P, 512], F32)) for b in range(8)]
        N_SUM = 6
        BZ, BN = 4, 6
        BG, BS = 6, 7
        L_AT, R_AT, C_AT = 0, 32, 64

        xln = nc.dram_tensor("xln", (ROWS, D), F32).ap()
        lists = nc.dram_tensor("lists", (SLOTS, 2), I32).ap()

        consts = sem("consts")
        const_ld = sem("const_ld")
        w_ld = [sem(f"w_ld{d}") for d in range(DC)]
        a_ld = [sem(f"a_ld{i}") for i in range(RING)]
        x_ld = [sem(f"x_ld{i}") for i in range(X_RING)]
        x2_ld = [sem(f"x2_ld{i}") for i in range(2)]
        row_ld = [sem(f"row_ld{i}") for i in range(3)]
        pre_st = sem("pre_st")
        pre_rdy = sem("pre_rdy")
        deg_done = sem("deg_done")
        mv_done = sem("mv_done")
        rstd_done = sem("rstd_done")
        dinv_done = sem("dinv_done")
        xn_done = sem("xn_done")
        nt_ready = sem("nt_ready")
        nt_hi_done = sem("nt_hi_done")
        nt_lo_done = sem("nt_lo_done")
        z_ready = sem("z_ready")
        zs_hi_done = sem("zs_hi_done")
        zs_lo_done = sem("zs_lo_done")
        a_eye = sem("a_eye")
        a_hi_done = sem("a_hi_done")
        a_lo_done = sem("a_lo_done")
        unit_done = sem("unit_done")
        bank_full = sem("bank_full")
        bank_read = sem("bank_read")
        w_hi_done = sem("w_hi_done")
        w_lo_done = sem("w_lo_done")
        gw1_ld = sem("gw1_ld")
        gw1_hi_done = sem("gw1_hi_done")
        gw1_lo_done = sem("gw1_lo_done")
        neg_done = sem("neg_done")
        exp_done = sem("exp_done")
        x1_done = sem("x1_done")
        mv2_done = sem("mv2_done")
        rstd2_done = sem("rstd2_done")
        xl_done = sem("xl_done")
        x1_st = [sem(f"x1_st{i}") for i in range(2)]
        xln_st = [sem(f"xln_st{i}") for i in range(2)]
        xt_ready = sem("xt_ready")
        xt_hi_done = sem("xt_hi_done")
        xt_lo_done = sem("xt_lo_done")
        g_ready = sem("g_ready")
        g_done = sem("g_done")
        l_ready = sem("l_ready")
        lc_done = sem("lc_done")
        le_done = sem("le_done")
        pd_done = sem("pd_done")
        pe2_done = sem("pe2_done")
        mask_done = sem("mask_done")
        r_ready = sem("r_ready")
        route_done = sem("route_done")
        list_st = [sem(f"list_st{q}") for q in range(2)]
        sched_done = sem("sched_done")
        dve_own = sem("dve_own")
        pool_own = sem("pool_own")
        phase1 = sem("phase1")
        early_done = sem("early_done")
        early_ld = sem("early_ld")
        lg_ld = sem("lg_ld")
        ly_ld = sem("ly_ld")
        w1_ld = [sem(f"w1_ld{i}") for i in range(4)]
        w2_ld = [sem(f"w2_ld{i}") for i in range(4)]
        be1_ld = sem("be1_ld")
        be2_ld = sem("be2_ld")
        xg_ld = sem("xg_ld")
        xe_ready = sem("xe_ready")
        xe_hi_done = sem("xe_hi_done")
        xe_lo_done = sem("xe_lo_done")
        w1_hi_done = sem("w1_hi_done")
        w1_lo_done = sem("w1_lo_done")
        w2_hi_done = sem("w2_hi_done")
        w2_lo_done = sem("w2_lo_done")
        h_ready = sem("h_ready")
        gelu_done = sem("gelu_done")
        h_hi_done = sem("h_hi_done")
        h_lo_done = sem("h_lo_done")
        w2_used = sem("w2_used")
        ye_ready = sem("ye_ready")
        yb_done = sem("yb_done")
        yw_done = sem("yw_done")
        y_add = sem("y_add")
        waited = sem("waited")

        units = [(j, c) for c in range(NCH) for j in range(NT)]
        NU = len(units)
        N_PAIR = NT // 2

        def chunk_tiles(c):
            return min(CT, NT - c * CT)

        def first(u):
            return units[u][0] == 0

        def closes(u):
            return units[u][0] == NT - 1

        def on_diagonal(u):
            j, c = units[u]
            return j // CT == c

        def bank_no(t):
            return t % N_SUM

        AHEAD = 2

        def last_unit(c):
            return (c + 1) * NT - 1

        pair_at, spread = {}, {}
        for p in range(N_PAIR):
            c = 2 * p // CT
            short = c + 1 == NCH - 1 and chunk_tiles(NCH - 1) <= CT // 2
            spread[p] = 1.5 if short else 1
            pair_at[p] = last_unit(c) + (p - c * CT // 2) * (6 if short else 12)
        STAGE = {"neg": 0, "elu0": 1, "elu1": 2, "norm0": 2, "norm1": 3, "xt0": 4, "xt1": 5,
                 "gate": 7, "logit": 9, "rank": 11}

        def stage_at(p, name):
            return pair_at[p] + int(STAGE[name] * spread[p])

        REACT = RING

        LAST = N_PAIR - 1

        def events(stages, shift, pairs=LAST):
            found = {}
            for p in range(pairs):
                for name, fn in stages:
                    found.setdefault(stage_at(p, name) + shift, []).append((fn, p))
            return found

        def run(found, u):
            for fn, p in found.pop(u, ()):
                fn(p)

        def finish(found):
            for u in sorted(found):
                run(found, u)

        def dinv(t):
            return rs[:, t, 1:2]

        def wait_unit(eng, u):
            j, c = units[u]
            if closes(u):
                eng.wait_ge(bank_full, c * CT + chunk_tiles(c))
            else:
                eng.wait_ge(unit_done, c * (NT - 1) + j + 1)

        def weights(s):
            return max(s - EARLY + 1, 0) if isinstance(s, int) else s - (EARLY - 1)

        block = ctx.enter_context(nc.Block())

        @block.sync
        def _(sp):
            def load_x(j):
                if j >= X_RING:
                    sp.wait_ge(xn_done, j - X_RING + 1)
                sp.dma_start(x_in[:, j % X_RING, :], x[j * P:(j + 1) * P, :]).then_inc(x_ld[j % X_RING], 16)

            def load_rows(j):
                for h in range(2):
                    n = 2 * j + h
                    if n >= 3:
                        sp.wait_ge(deg_done, n - 2)
                    sp.dma_start(row_in[:, n % 3, :], adj[j * P:(j + 1) * P, h * HALF:(h + 1) * HALF])\
                      .then_inc(row_ld[n % 3], 16)

            def load_unit(u):
                j, c = units[u]
                if u >= RING:
                    sp.wait_ge(a_lo_done, u - RING + 1)
                n = chunk_tiles(c) * P
                sp.dma_start(a_raw[:, u % RING, 0:n],
                             adj_t[j * P:(j + 1) * P, c * CW:c * CW + n]).then_inc(a_ld[u % RING], 16)

            def load_pair_x(p):
                for q in range(2):
                    if p == 0:
                        sp.wait_ge(xn_done, NT)
                    else:
                        sp.wait_ge(x1_st[q], 16 * p)
                        sp.wait_ge(xl_done, 2 * p - 1 + q)
                    t = 2 * p + q
                    sp.dma_start(x_in[:, q, :], x[t * P:(t + 1) * P, :]).then_inc(x2_ld[q], 16)

            sp.dma_start(x_in[:, 0, :], x[0:P, :]).then_inc(x_ld[0], 16)
            for d in range(DC):
                sp.dma_start(w_raw[:, d, :], w[d * P:(d + 1) * P, :]).then_inc(w_ld[d], 16)
            load_x(1)
            load_x(2)
            for it in range(-4, NT):
                load_unit(it + 4)
                if X_RING <= it + 6 < NT:
                    load_x(it + 6)
                if 0 <= it + 3 < NT:
                    load_rows(it + 3)
                if it == 0:
                    sp.dma_start(gw2_sb[:, :, :], gw2.rearrange("(c p) n -> p c n", p=P)).then_inc(const_ld, 16)
                    sp.dma_start(gb1_sb[:, :], gb1).then_inc(const_ld, 16)
                    sp.dma_start(gb2_sb[:, :], gb2.partition_broadcast(P)).then_inc(const_ld, 16)
            sp.wait_ge(deg_done, 2 * NT)
            sp.dma_start(gw1_raw[:, :, :], gw1.rearrange("(c p) n -> p c n", p=P)).then_inc(gw1_ld, 16)
            post = events([("elu0", load_pair_x)], RING, N_PAIR)
            for u in range(NT + 4, NU):
                run(post, u)
                load_unit(u)
            finish(post)

            def load_weights(ex, new, m, src, dst, ld):
                if src is we1:
                    d, w_e = dst[:, :, m * 256:(m + 1) * 256], src[bass.ds(ex, 1), :, m * 256:(m + 1) * 256]
                else:
                    d, w_e = dst[:, 2 * m:2 * m + 2, :], src[bass.ds(ex, 1), m * 256:(m + 1) * 256, :]
                sp.dma_start(d, w_e.rearrange("o (c p) n -> p (o c) n", p=P), cond=new).then_inc(ld[m], 16)

            def load_be1(ex):
                sp.dma_start(be1_sb[:, :], be1[bass.ds(ex, 1), :, :]
                             .rearrange("o p n -> (o p) n")).then_inc(be1_ld, 16)

            sp.wait_ge(early_done, 1)
            wait_unit(sp, last_unit(NCH - 2) + 16)
            ex = sp.value_load(early[0:1, 1:2], min_val=0, max_val=E - 1)
            for m in range(4):
                load_weights(ex, None, m, we1, w1_raw, w1_ld)
            load_be1(ex)
            for m in range(4):
                load_weights(ex, None, m, we2, w2_raw, w2_ld)
            sp.wait_ge(phase1, 2)

            with sp.Fori(EARLY, STEPS) as s:
                row = sp.value_load(sched[0:1, s, 0:1], min_val=0, max_val=SLOTS - S_ROWS)
                ex = sp.value_load(sched[0:1, s, 1:2], min_val=0, max_val=E - 1)
                new = sp.value_load(sched[0:1, s, 2:3], min_val=0, max_val=1)
                sp.wait_ge(xg_ld, 32 * s)
                sp.dma_start(list_g[:, :, :], lists[bass.ds(row, S_ROWS), :]
                             .rearrange("(p j) c -> p j c", p=P)).then_inc(lg_ld, 16)
                for m in range(4):
                    sp.wait_ge(w1_lo_done, 4 * (weights(s) - 1) + m + 1)
                    load_weights(ex, new, m, we1, w1_raw, w1_ld)
                sp.wait_ge(gelu_done, HC * s)
                load_be1(ex)
                for m in range(4):
                    sp.wait_ge(w2_lo_done, 4 * (weights(s) - 1) + m + 1)
                    load_weights(ex, new, m, we2, w2_raw, w2_ld)

        @block.gpsimd
        def _(pool):
            own = [0]

            def link(ins):
                own[0] += 1
                ins.then_inc(pool_own, 1)
                pool.wait_ge(pool_own, own[0])

            pool.memset(ident[:, :], 0.0).then_inc(pool_own, 1)
            pool.memset(ones[:, :], 1.0).then_inc(pool_own, 1)
            pool.memset(ones_bf[:, :], 1.0).then_inc(pool_own, 1)
            pool.memset(ln_add[:, 0:1], EPS).then_inc(pool_own, 1)
            pool.memset(ln_add[:, 1:2], 1.0).then_inc(pool_own, 1)
            pool.memset(ln_pow[:, :], -0.5).then_inc(pool_own, 1)
            own[0] = 6
            pool.wait_ge(pool_own, own[0])
            link(pool.affine_select(out=ident[:, :], in_=ident[:, :], compare_op=ALU.not_equal, fill=1.0,
                                    base=0, pattern=[[-1, P]], channel_multiplier=1))
            pool.nop().then_inc(consts, 1)

            def rstd(j):
                k = j % 2
                pool.wait_ge(mv_done, j + 1)
                link(pool.tensor_tensor(pk[:, k, 0:1], mv[:, j, 1:2], ln_add[:, 0:1], ALU.add))
                pool.tensor_tensor(rs[:, j, 0:1], pk[:, k, 0:1], ln_pow[:, 0:1], ALU.pow).then_inc(rstd_done, 1)

            def dinv_make(j):
                k = j % 2
                pool.wait_ge(deg_done, 2 * j + 2)
                link(pool.tensor_tensor(deg1[:, k, :], deg[:, j, 0:1], deg[:, j, 1:2], ALU.add))
                link(pool.tensor_tensor(pk[:, k, 1:2], deg1[:, k, :], ln_add[:, 1:2], ALU.add))
                pool.tensor_tensor(rs[:, j, 1:2], pk[:, k, 1:2], ln_pow[:, 1:2], ALU.pow).then_inc(dinv_done, 1)

            def add_eye(u):
                j, c = units[u]
                a = a_raw[:, u % RING, j % CT * P:(j % CT + 1) * P]
                pool.wait_ge(a_ld[u % RING], 16 * (u // RING + 1))
                pool.tensor_tensor(a, a, ident[:, :], ALU.add).then_inc(a_eye, 1)

            def norm2(p, q):
                for t in (2 * p + q,):
                    pool.wait_ge(mv2_done, t + 1)
                    link(pool.tensor_tensor(pk2[:, q, :], mv2[:, q, 1:2], ln_add[:, 0:1], ALU.add))
                    pool.tensor_tensor(rstd2[:, q, :], pk2[:, q, :], ln_pow[:, 0:1], ALU.pow).then_inc(rstd2_done, 1)
                    pool.dma_start(out[t * P:(t + 1) * P, :], x_in[:, q, :]).then_inc(x1_st[q], 16)

            def store_rows(p, q):
                for t in (2 * p + q,):
                    pool.wait_ge(xl_done, t + 1)
                    pool.dma_start(xln[t * P:(t + 1) * P, :], x_n[:, q, :]).then_inc(xln_st[q], 16)

            def scatter_lists(p):
                pool.wait_ge(route_done, p + 1)
                if p == 0:
                    pool.wait_ge(pre_st, 64)
                for q in range(2):
                    for k in range(TOP_K):
                        pool.indirect_dma_start(
                            out=lists[:, :], out_offset=bass.IndirectOffsetOnAxis(
                                ap=slot[:, p % 2, q, k:k + 1].bitcast(U32), axis=0),
                            in_=pay[:, p % 2, q, k, :], in_offset=None).then_inc(list_st[p % 2], 16)

            rstd(0)
            rstd(1)
            rstd(2)
            link(pool.affine_select(out=upper[:, :], in_=ones_bf[:, :], compare_op=ALU.is_gt, fill=0.0,
                                    base=0, pattern=[[1, P]], channel_multiplier=-1))
            link(pool.iota(cols8[:, :], [[1, E]], base=0, channel_multiplier=0,
                           allow_small_or_imprecise_dtypes=True))
            link(pool.iota(base0[:, :], [[CAP, E]], base=0, channel_multiplier=0,
                           allow_small_or_imprecise_dtypes=True))
            link(pool.iota(s_i[:, :], [[1, STEPS]], base=-EARLY, channel_multiplier=0,
                           allow_small_or_imprecise_dtypes=True))
            link(pool.iota(tok_id[:, :], [[P, NT]], base=0, channel_multiplier=1))
            link(pool.iota(pre[:, :, 0], [[1, PRE]], base=0, channel_multiplier=PRE))
            link(pool.memset(zrow[:, :, :], 0.0))
            pool.nop().then_inc(consts, 1)




            for it in range(-2, NT):
                if it == 2:
                    for r in (NP, 2 * LAST * P):
                        pool.dma_start(xln[r:r + SJ * P, :].rearrange("(j p) n -> p j n", p=P),
                                       zrow[:, :, :]).then_inc(pre_st, 16)
                    pool.dma_start(out[NP:ROWS, :].rearrange("(j p) n -> p j n", p=P), zrow[:, :, :]).then_inc(pre_st, 16)
                    pool.wait_ge(pre_rdy, 1)
                    pool.dma_start(lists.rearrange("(p c) k -> p c k", p=P), pre[:, :, :]).then_inc(pre_st, 16)
                if on_diagonal(it + 2):
                    add_eye(it + 2)
                if 3 <= it + 4 < NT:
                    rstd(it + 4)
                if it + 2 < NT:
                    dinv_make(it + 2)
            work = []
            for u in range(NT + 2, NU):
                if on_diagonal(u):
                    work.append((u, 0, add_eye, (u,)))
            for p in range(LAST):
                work.append((stage_at(p, "norm0") + REACT, 2, norm2, (p, 0)))
                work.append((stage_at(p, "norm1") + REACT, 2, norm2, (p, 1)))
                work.append((stage_at(p, "xt0") + REACT - 1, 3, store_rows, (p, 0)))
                work.append((stage_at(p, "xt1") + REACT - 1, 3, store_rows, (p, 1)))
                work.append((stage_at(p, "rank") + REACT, 4, scatter_lists, (p,)))
            for _, _, fn, args in sorted(work, key=lambda v: v[:2]):
                fn(*args)
            def load_be2(ex):
                pool.dma_start(be2_sb[:, :], be2[bass.ds(ex, 1), :]
                               .rearrange("o n -> (o n)").partition_broadcast(P)).then_inc(be2_ld, 16)

            def load_for_y(s):
                row = pool.value_load(sched[0:1, s, 0:1], min_val=0, max_val=SLOTS - S_ROWS)
                ex = pool.value_load(sched[0:1, s, 1:2], min_val=0, max_val=E - 1)
                pool.dma_start(list_y[:, :, :], lists[bass.ds(row, S_ROWS), :]
                               .rearrange("(p j) c -> p j c", p=P)).then_inc(ly_ld, 16)
                load_be2(ex)

            def gather(s):
                if isinstance(s, int) and s < EARLY:
                    tokens = list_e[:, s, :, :]
                else:
                    tokens = list_g
                    pool.wait_ge(lg_ld, 16 * (s - EARLY + 1))
                if not (isinstance(s, int) and s == 0):
                    pool.wait_ge(xe_ready, SJ * s)
                pool.sem_inc(waited, 1)
                for jj in range(SJ):
                    pool.indirect_dma_start(
                        out=x_g[:, jj, :], out_offset=None, in_=xln[:, :],
                        in_offset=bass.IndirectOffsetOnAxis(
                            ap=tokens[:, jj, 0:1].bitcast(U32), axis=0)).then_inc(xg_ld, 16)

            def add_rows(s):
                tokens = list_e[:, s, :, :] if isinstance(s, int) and s < EARLY else list_y
                for jj in range(SJ):
                    pool.wait_ge(yw_done, SJ * s + jj + 1)
                    pool.sem_inc(waited, 1)
                    pool.indirect_dma_start(
                        out=out[:, :], out_offset=bass.IndirectOffsetOnAxis(
                            ap=tokens[:, jj, 0:1].bitcast(U32), axis=0),
                        in_=y_sb[:, jj, :], in_offset=None, compute_op=ALU.add).then_inc(y_add, 16)
                    pool.wait_ge(y_add, 16 * (SJ * s + jj + 1))

            norm2(LAST, 0)
            norm2(LAST, 1)
            for q in range(2):
                pool.wait_ge(list_st[q], 16 * 2 * TOP_K * ((LAST + 1 - q) // 2))
                pool.wait_ge(xln_st[q], 16 * LAST)
            pool.wait_ge(early_done, 1)
            row = pool.value_load(early[0:1, 0:1], min_val=0, max_val=SLOTS - EARLY * S_ROWS)
            pool.dma_start(list_e[:, :, :, :], lists[bass.ds(row, EARLY * S_ROWS), :]
                           .rearrange("(s p j) c -> p s j c", s=EARLY, p=P)).then_inc(early_ld, 16)
            pool.wait_ge(early_ld, 16)
            gather(0)
            pool.wait_ge(xg_ld, 16 * SJ)
            store_rows(LAST, 0)
            store_rows(LAST, 1)
            for q in range(2):
                pool.wait_ge(xln_st[q], 16 * N_PAIR)
            gather(1)
            load_be2(pool.value_load(early[0:1, 1:2], min_val=0, max_val=E - 1))
            scatter_lists(LAST)
            for q in range(2):
                pool.wait_ge(list_st[q], 16 * 2 * TOP_K * ((N_PAIR + 1 - q) // 2))
                pool.wait_ge(x1_st[q], 16 * N_PAIR)
            pool.nop().then_inc(phase1, 1)
            pool.wait_ge(phase1, 2)

            gather(EARLY)
            for s in range(EARLY - 1):
                add_rows(s)
            gather(EARLY + 1)
            add_rows(EARLY - 1)
            load_for_y(EARLY)
            with pool.Fori(EARLY + 1, STEPS - 1) as s:
                gather(s + 1)
                add_rows(s - 1)
                load_for_y(s)
            add_rows(STEPS - 2)
            load_for_y(STEPS - 1)
            add_rows(STEPS - 1)

        @block.scalar
        def _(act):
            def evac_sums(c):
                for i in range(chunk_tiles(c)):
                    t = c * CT + i
                    act.wait_ge(bank_full, t + 1)
                    act.wait_ge(dinv_done, NT)
                    if t >= Y_RING:
                        act.wait_ge(x1_done, t - Y_RING + 1)
                    act.activation(y_raw[:, t % Y_RING, :], bank[bank_no(t)][:, :], ACT.Copy,
                                   scale=dinv(t)).then_inc(bank_read, 1)

            def exp_neg(p, q):
                t = 2 * p + q
                act.wait_ge(neg_done, t + 1)
                act.activation(e_neg[:, q, :], e_neg[:, q, :], ACT.Exp).then_inc(exp_done, 1)

            def evac_xt(p, q):
                act.wait_ge(xt_ready, 2 * p + q + 1)
                act.activation(xt_hi[:, :, q * P:(q + 1) * P],
                               bank[BG][:, :].rearrange("p (c n) -> p c n", c=DC),
                               ACT.Copy).then_inc(xt_hi_done, 1)

            def relu_gate(p):
                act.wait_ge(g_ready, p + 1)
                act.wait_ge(const_ld, 48)
                for hb in range(GC):
                    act.activation(g_t[:, hb, :], bank[BG][:, hb * 256:(hb + 1) * 256], ACT.Relu,
                                   bias=gb1_sb[:, hb:hb + 1]).then_inc(g_done, 1)

            def exp_logits(p):
                act.wait_ge(lc_done, p + 1)
                act.activation(le[:, :, :], lc[:, :, :], ACT.Exp).then_inc(le_done, 1)
                act.wait_ge(pd_done, p + 1)
                act.activation(pe2[:, :], pd[:, :], ACT.Exp).then_inc(pe2_done, 1)

            def split_gw1(_):
                act.wait_ge(gw1_ld, 16)
                act.activation(gw1_hi[:, :, :], gw1_raw[:, :, :], ACT.Copy).then_inc(gw1_hi_done, 1)

            post = events([("elu0", lambda p: exp_neg(p, 0)), ("elu1", lambda p: exp_neg(p, 1)),
                           ("xt0", lambda p: evac_xt(p, 0)), ("xt1", lambda p: evac_xt(p, 1)),
                           ("gate", relu_gate), ("logit", exp_logits)], REACT)
            for c in range(NCH):
                post.setdefault(last_unit(c) + RING, []).insert(0, (evac_sums, c))
            post.setdefault(NT + 6, []).append((split_gw1, None))

            def degree(j):
                for n in (2 * j, 2 * j + 1):
                    act.wait_ge(row_ld[n % 3], 16 * (n // 3 + 1))
                    act.activation(row_in[:, n % 3, :], row_in[:, n % 3, :], ACT.Copy,
                                   accum_out=deg[:, j, n % 2:n % 2 + 1]).then_inc(deg_done, 1)

            def nt_split(j):
                act.wait_ge(nt_ready, j + 1)
                if j >= 2:
                    act.wait_ge(z_ready, j - 1)
                act.activation(nt_hi[:, j % 2, :, :], bank[BN + j % 2][:, :].rearrange("p (c n) -> p c n", c=DC),
                               ACT.Copy).then_inc(nt_hi_done, 1)

            def zs_split(j):
                act.wait_ge(z_ready, j + 1)
                act.wait_ge(dinv_done, j + 1)
                if j == NT - 1:
                    act.wait_ge(pre_st, 64)
                act.activation(zs_hi[:, j, :], bank[BZ + j % 2][:, :], ACT.Copy, scale=dinv(j)).then_inc(zs_hi_done, 1)

            def a_split(u):
                n = chunk_tiles(units[u][1]) * P
                act.wait_ge(a_ld[u % RING], 16 * (u // RING + 1))
                if on_diagonal(u):
                    act.wait_ge(a_eye, sum(on_diagonal(v) for v in range(u + 1)))
                if u >= RING:
                    wait_unit(act, u - RING)
                act.activation(a_hi[:, u % RING, 0:n], a_raw[:, u % RING, 0:n], ACT.Copy).then_inc(a_hi_done, 1)

            for d in range(DC):
                act.wait_ge(w_ld[d], 16)
                act.activation(w_hi[:, d, :], w_raw[:, d, :], ACT.Copy).then_inc(w_hi_done, 1)
            for it in range(-2, NT):
                if it + 2 < NT:
                    nt_split(it + 2)
                a_split(it + 2)
                if 0 <= it + 1 < NT:
                    zs_split(it + 1)
                if it + 2 < NT:
                    degree(it + 2)
            for u in range(NT + 2, NU):
                run(post, u)
                a_split(u)
            finish(post)

            def w1_split(s, m, first):
                act.wait_ge(w1_ld[m], 16 * weights(s) + 16)
                if not first:
                    act.wait_ge(h_ready, HC * (s - 1) + 2 * m + 2)
                act.activation(w1_hi[:, :, m * 256:(m + 1) * 256], w1_raw[:, :, m * 256:(m + 1) * 256],
                               ACT.Copy).then_inc(w1_hi_done, 1)

            def w2_split(s, m, first):
                act.wait_ge(w2_ld[m], 16 * weights(s) + 16)
                if not first:
                    if m < 3:
                        act.wait_ge(w2_used, 3 * (s - 1) + m + 1)
                    else:
                        act.wait_ge(ye_ready, SJ * s)
                act.activation(w2_hi[:, 2 * m:2 * m + 2, :], w2_raw[:, 2 * m:2 * m + 2, :],
                               ACT.Copy).then_inc(w2_hi_done, 1)

            def xe_split(s):
                for jj in range(SJ):
                    act.wait_ge(xe_ready, SJ * s + jj + 1)
                    act.activation(xe_hi[:, :, jj * P:(jj + 1) * P],
                                   bank[jj][:, :].rearrange("p (c n) -> p c n", c=DC),
                                   ACT.Copy).then_inc(xe_hi_done, 1)

            def step(s, rows, new):
                act.wait_ge(be1_ld, 16 * weights(s) + 16)
                for m in range(4):
                    hb = bank[2 + m]
                    act.wait_ge(h_ready, HC * s + 2 * m + 2)
                    for k in range(2):
                        act.activation(hb[:, k * 256:(k + 1) * 256], hb[:, k * 256:(k + 1) * 256], ACT.Gelu,
                                       bias=be1_sb[:, 2 * m + k:2 * m + k + 1]).then_inc(gelu_done, 1)
                    act.wait_ge(gelu_done, HC * s + 2 * m + 2)
                    act.activation(h_hi[:, 2 * m:2 * m + 2, :], hb[:, :].rearrange("p (k n) -> p k n", k=2),
                                   ACT.Copy).then_inc(h_hi_done, 1)
                    if new:
                        w1_split(s + 1, m, False)
                if rows:
                    xe_split(s + 1)
                if new:
                    for m in range(4):
                        w2_split(s + 1, m, False)

            exp_neg(LAST, 0)
            exp_neg(LAST, 1)
            act.wait_ge(bank_full, NT)
            for m in range(4):
                w1_split(0, m, True)
                if m < 2:
                    evac_xt(LAST, m)
            xe_split(0)
            relu_gate(LAST)
            exp_logits(LAST)
            for m in range(4):
                w2_split(0, m, True)
            for s in range(EARLY - 1):
                step(s, True, False)
            step(EARLY - 1, True, True)
            with act.Fori(EARLY, STEPS - 1) as s:
                step(s, True, True)
            step(STEPS - 1, False, False)

        @block.vector
        def _(dve):
            own = [0]

            def link(ins):
                own[0] += 1
                ins.then_inc(dve_own, 1)
                dve.wait_ge(dve_own, own[0])

            def stats(j):
                dve.wait_ge(x_ld[j % X_RING], 16 * (j // X_RING + 1))
                link(dve.bn_stats(stat6[:, j % 2, :], x_in[:, j % X_RING, :]))
                dve.bn_aggr(mv[:, j, :], stat6[:, j % 2, :]).then_inc(mv_done, 1)

            def x_norm(j):
                dve.wait_ge(rstd_done, j + 1)
                dve.wait_ge(mv_done, j + 1)
                if j >= 2:
                    dve.wait_ge(nt_ready, j - 1)
                dve.tensor_scalar(x_n[:, j % 2, :], x_in[:, j % X_RING, :], mv[:, j, 0:1], rs[:, j, 0:1],
                                  ALU.subtract, ALU.mult).then_inc(xn_done, 1)

            def nt_rest(j):
                dve.wait_ge(nt_hi_done, j + 1)
                dve.tensor_tensor(nt_lo[:, j % 2, :, :], bank[BN + j % 2][:, :].rearrange("p (c n) -> p c n", c=DC),
                                  nt_hi[:, j % 2, :, :].bitcast(F32), ALU.subtract).then_inc(nt_lo_done, 1)

            def zs_rest(j):
                dve.wait_ge(zs_hi_done, j + 1)
                if j == NT - SJ:
                    dve.wait_ge(pre_st, 64)
                dve.scalar_tensor_tensor(zs_lo[:, j, :], bank[BZ + j % 2][:, :], dinv(j),
                                         zs_hi[:, j, :].bitcast(F32), ALU.mult, ALU.subtract).then_inc(zs_lo_done, 1)

            def a_rest(u):
                n = chunk_tiles(units[u][1]) * P
                dve.wait_ge(a_hi_done, u + 1)
                dve.tensor_tensor(a_lo[:, u % RING, 0:n], a_raw[:, u % RING, 0:n],
                                  a_hi[:, u % RING, 0:n].bitcast(F32), ALU.subtract).then_inc(a_lo_done, 1)

            def neg_part(p, q):
                t = 2 * p + q
                dve.wait_ge(bank_read, t + 1)
                dve.tensor_scalar(e_neg[:, q, :], y_raw[:, t % Y_RING, :], 0.0, None, ALU.min).then_inc(neg_done, 1)

            def elu(p, q):
                t = 2 * p + q
                y = y_raw[:, t % Y_RING, :]
                dve.wait_ge(exp_done, t + 1)
                link(dve.scalar_tensor_tensor(y, e_neg[:, q, :], -1.0, y, ALU.add, ALU.max))
                dve.wait_ge(x2_ld[q], 16 * (p + 1))
                dve.tensor_tensor(x_in[:, q, :], y, x_in[:, q, :], ALU.add).then_inc(x1_done, 1)
                dve.wait_ge(x1_done, t + 1)
                link(dve.bn_stats(stat6[:, q, :], x_in[:, q, :]))
                dve.bn_aggr(mv2[:, q, :], stat6[:, q, :]).then_inc(mv2_done, 1)

            def norm(p, q):
                t = 2 * p + q
                dve.wait_ge(rstd2_done, t + 1)
                dve.wait_ge(mv2_done, t + 1)
                if p > 0:
                    dve.wait_ge(xln_st[q], 16 * p)
                dve.tensor_scalar(x_n[:, q, :], x_in[:, q, :], mv2[:, q, 0:1], rstd2[:, q, :],
                                  ALU.subtract, ALU.mult).then_inc(xl_done, 1)

            def xt_rest(p, q):
                dve.wait_ge(xt_hi_done, 2 * p + q + 1)
                dve.tensor_tensor(xt_lo[:, :, q * P:(q + 1) * P],
                                  bank[BG][:, :].rearrange("p (c n) -> p c n", c=DC),
                                  xt_hi[:, :, q * P:(q + 1) * P].bitcast(F32),
                                  ALU.subtract).then_inc(xt_lo_done, 1)

            def experts(p):
                dve.wait_ge(l_ready, p + 1)
                dve.wait_ge(const_ld, 48)
                link(dve.tensor_tensor(lg[:, :, :], bank[BS][:, L_AT:L_AT + 2 * E].rearrange("p (q e) -> p q e", q=2),
                                       gb2_sb[:, :].unsqueeze(1).to_broadcast([P, 2, E]), ALU.add))
                link(dve.tensor_reduce(lmax[:, :], lg[:, :, :], AX.X, ALU.max))
                dve.tensor_tensor(lc[:, :, :], lg[:, :, :], lmax[:, :].unsqueeze(2).to_broadcast([P, 2, E]),
                                  ALU.subtract).then_inc(lc_done, 1)
                dve.wait_ge(le_done, p + 1)
                link(dve.tensor_reduce(lsum[:, :], le[:, :, :], AX.X, ALU.add))
                link(dve.reciprocal(lrec[:, :], lsum[:, :]))
                link(dve.tensor_tensor(prob[:, :, :], le[:, :, :], lrec[:, :].unsqueeze(2).to_broadcast([P, 2, E]),
                                       ALU.mult))
                for q in range(2):
                    link(dve.max(top[:, q, :], prob[:, q, :]))
                dve.tensor_tensor(pd[:, :], top[:, :, 1], top[:, :, 0], ALU.subtract).then_inc(pd_done, 1)
                for q in range(2):
                    link(dve.max_index(topi[:, q, :], top[:, q, :], prob[:, q, :]))
                link(dve.tensor_copy(topf[:, :, :], topi[:, :, :]))
                for q in range(2):
                    for k in range(TOP_K):
                        link(dve.tensor_scalar(hot[:, q, k, :], cols8[:, :], topf[:, q, k:k + 1], None, ALU.is_equal))
                dve.tensor_tensor(mask[:, :, :], hot[:, :, 0, :], hot[:, :, 1, :], ALU.add).then_inc(mask_done, 1)
                dve.wait_ge(pe2_done, p + 1)
                link(dve.tensor_scalar(pden[:, :], pe2[:, :], 1.0, None, ALU.add))
                link(dve.reciprocal(wts[:, :, 0], pden[:, :]))
                link(dve.tensor_tensor(wts[:, :, 1], wts[:, :, 0], pe2[:, :], ALU.mult))

            def slots(p):
                b = p % 2
                dve.wait_ge(r_ready, p + 1)
                link(dve.tensor_tensor(rb[:, :, :], bank[BS][:, R_AT:R_AT + 2 * E].rearrange("p (q e) -> p q e", q=2),
                                       base[:, :].unsqueeze(1).to_broadcast([P, 2, E]), ALU.add))
                link(dve.tensor_tensor(pick[:, :, :, :], hot[:, :, :, :],
                                       rb[:, :, :].unsqueeze(2).to_broadcast([P, 2, TOP_K, E]), ALU.mult))
                link(dve.tensor_reduce(slotf[:, :, :], pick[:, :, :, :], AX.X, ALU.add))
                if p >= 2:
                    dve.wait_ge(list_st[b], 16 * 2 * TOP_K * (p // 2))
                link(dve.tensor_copy(slot[:, b, :, :], slotf[:, :, :]))
                link(dve.tensor_copy(pay[:, b, :, :, 0],
                                     tok_id[:, 2 * p:2 * p + 2].unsqueeze(2).to_broadcast([P, 2, TOP_K])))
                link(dve.tensor_copy(pay[:, b, :, :, 1].bitcast(F32), wts[:, :, :]))
                dve.tensor_tensor(base[:, :], base[:, :], bank[BS][:, C_AT:C_AT + E], ALU.add).then_inc(route_done, 1)
                dve.wait_ge(route_done, p + 1)

            def gw1_rest(_):
                dve.wait_ge(gw1_hi_done, 1)
                dve.tensor_tensor(gw1_lo[:, :, :], gw1_raw[:, :, :], gw1_hi[:, :, :].bitcast(F32),
                                  ALU.subtract).then_inc(gw1_lo_done, 1)

            post = events([("neg", lambda p: (neg_part(p, 0), neg_part(p, 1))),
                           ("elu0", lambda p: elu(p, 0)), ("elu1", lambda p: elu(p, 1)),
                           ("norm0", lambda p: norm(p, 0)), ("norm1", lambda p: norm(p, 1)),
                           ("xt0", lambda p: xt_rest(p, 0)), ("xt1", lambda p: xt_rest(p, 1)),
                           ("logit", experts), ("rank", slots)], REACT)
            post.setdefault(NT + 6, []).append((gw1_rest, None))

            stats(0)
            x_norm(0)
            stats(1)
            for it in range(-2, NT):
                if it + 3 < NT:
                    x_norm(it + 3)
                if it + 4 < NT:
                    stats(it + 4)
                if it == -2:
                    for d in range(DC):
                        dve.wait_ge(w_hi_done, d + 1)
                        dve.tensor_tensor(w_lo[:, d, :], w_raw[:, d, :], w_hi[:, d, :].bitcast(F32),
                                          ALU.subtract).then_inc(w_lo_done, 1)
                if 0 <= it + 2 < NT:
                    nt_rest(it + 2)
                if it + 2 >= 0:
                    a_rest(it + 2)
                if 0 <= it + 1 < NT:
                    zs_rest(it + 1)
                if it == 0:
                    dve.wait_ge(consts, 2)
                    link(dve.tensor_scalar(pre[:, :, 0], pre[:, :, 0], S_ROWS - 1, None, ALU.bitwise_and))
                    link(dve.tensor_scalar(pre[:, :, 0], pre[:, :, 0], float(DUMMY), None, ALU.add))
                    link(dve.memset(pre[:, :, 1], 0))
                    dve.nop().then_inc(pre_rdy, 1)
                    link(dve.tensor_copy(base[:, :], base0[:, :]))
            for u in range(NT + 2, NU):
                run(post, u)
                a_rest(u)
            finish(post)

            link(dve.tensor_tensor(cnt[:, :], base[:, :], base0[:, :], ALU.subtract))
            link(dve.max(most[:, :], cnt[:, :]))
            link(dve.max_index(most_i[:, :], most[:, :], cnt[:, :]))
            link(dve.tensor_copy(e_star[:, 1:2], most_i[:, 0:1]))
            link(dve.tensor_scalar(e_star[:, 0:1], e_star[:, 1:2], float(CAP), None, ALU.mult))
            dve.tensor_copy(early[:, :], e_star[:, :]).then_inc(early_done, 1)

            def w1_rest(s, m):
                dve.wait_ge(w1_hi_done, 4 * weights(s) + m + 1)
                dve.tensor_tensor(w1_lo[:, :, m * 256:(m + 1) * 256], w1_raw[:, :, m * 256:(m + 1) * 256],
                                  w1_hi[:, :, m * 256:(m + 1) * 256].bitcast(F32),
                                  ALU.subtract).then_inc(w1_lo_done, 1)

            def w2_rest(s, m):
                dve.wait_ge(w2_hi_done, 4 * weights(s) + m + 1)
                dve.tensor_tensor(w2_lo[:, 2 * m:2 * m + 2, :], w2_raw[:, 2 * m:2 * m + 2, :],
                                  w2_hi[:, 2 * m:2 * m + 2, :].bitcast(F32),
                                  ALU.subtract).then_inc(w2_lo_done, 1)

            def xe_rest(s):
                for jj in range(SJ):
                    dve.wait_ge(xe_hi_done, SJ * s + jj + 1)
                    dve.tensor_tensor(xe_lo[:, :, jj * P:(jj + 1) * P],
                                      bank[jj][:, :].rearrange("p (c n) -> p c n", c=DC),
                                      xe_hi[:, :, jj * P:(jj + 1) * P].bitcast(F32),
                                      ALU.subtract).then_inc(xe_lo_done, 1)

            def weigh(s, first):
                dve.wait_ge(be2_ld, 16 * weights(s) + 16)
                if isinstance(s, int) and s < EARLY:
                    dve.wait_ge(early_ld, 16)
                    slots_y = list_e[:, s, :, :]
                else:
                    dve.wait_ge(ly_ld, 16 * (s - EARLY + 1))
                    slots_y = list_y
                for jj in range(SJ):
                    dve.wait_ge(ye_ready, SJ * s + jj + 1)
                    if not first:
                        dve.wait_ge(y_add, 16 * (SJ * (s - 1) + jj + 1))
                    dve.tensor_tensor(y_sb[:, jj, :], bank[6 + jj][:, :], be2_sb[:, :], ALU.add).then_inc(yb_done, 1)
                    dve.wait_ge(yb_done, SJ * s + jj + 1)
                    dve.tensor_scalar(y_sb[:, jj, :], y_sb[:, jj, :], slots_y[:, jj, 1:2].bitcast(F32), None,
                                      ALU.mult).then_inc(yw_done, 1)

            def step(s, rows, new, earlier):
                for m in range(4):
                    dve.wait_ge(h_hi_done, 4 * s + m + 1)
                    dve.tensor_tensor(h_lo[:, 2 * m:2 * m + 2, :], bank[2 + m][:, :].rearrange("p (k n) -> p k n", k=2),
                                      h_hi[:, 2 * m:2 * m + 2, :].bitcast(F32), ALU.subtract).then_inc(h_lo_done, 1)
                    if m == 0 and earlier > 0:
                        weigh(s - 1, earlier == 1)
                    if new:
                        w1_rest(s + 1, m)
                if rows:
                    xe_rest(s + 1)
                if new:
                    for m in range(4):
                        w2_rest(s + 1, m)

            def schedule():
                link(dve.tensor_tensor(cnt[:, :], base[:, :], base0[:, :], ALU.subtract))
                link(dve.tensor_scalar(tiles_i[:, :], cnt[:, :], float(S_ROWS - 1), None, ALU.add))
                link(dve.tensor_scalar(tiles_i[:, :], tiles_i[:, :], S_ROWS.bit_length() - 1, None,
                                       ALU.logical_shift_right))
                link(dve.tensor_copy(tiles_f[:, :], tiles_i[:, :]))
                link(dve.tensor_scalar(e_hot[:, :], cols8[:, :], e_star[:, 1:2], float(EARLY), ALU.is_equal, ALU.mult))
                link(dve.tensor_tensor(tiles_f[:, :], tiles_f[:, :], e_hot[:, :], ALU.subtract))
                link(dve.tensor_copy(cum[:, 0, :], tiles_f[:, :]))
                for n, d in enumerate((1, 2, 4)):
                    link(dve.tensor_copy(cum[:, n + 1, 0:d], cum[:, n, 0:d]))
                    link(dve.tensor_tensor(cum[:, n + 1, d:E], cum[:, n, d:E], cum[:, n, 0:E - d], ALU.add))
                link(dve.tensor_tensor(past[:, :, :], cum[:, 3, :].unsqueeze(1).to_broadcast([P, STEPS, E]),
                                       s_i[:, :].unsqueeze(2).to_broadcast([P, STEPS, E]), ALU.is_le))
                link(dve.tensor_tensor(past_t[:, :, :], past[:, :, :],
                                       tiles_f[:, :].unsqueeze(1).to_broadcast([P, STEPS, E]), ALU.mult))
                link(dve.tensor_reduce(s_e[:, :], past[:, :, :], AX.X, ALU.add))
                link(dve.tensor_reduce(s_t[:, :], past_t[:, :, :], AX.X, ALU.add))
                link(dve.tensor_tensor(s_t[:, :], s_i[:, :], s_t[:, :], ALU.subtract))
                link(dve.tensor_scalar(s_t[:, :], s_t[:, :], float(S_ROWS), None, ALU.mult))
                link(dve.tensor_scalar(s_r[:, :, 1], s_e[:, :], float(E - 1), None, ALU.min))
                link(dve.tensor_scalar(s_r[:, :, 0], s_e[:, :], float(CAP), None, ALU.mult))
                link(dve.tensor_tensor(s_r[:, :, 0], s_r[:, :, 0], s_t[:, :], ALU.add))
                link(dve.tensor_scalar(e_row[:, :], s_e[:, :], e_star[:, 1:2], float(EARLY * S_ROWS),
                                       ALU.is_equal, ALU.mult))
                link(dve.tensor_tensor(s_r[:, :, 0], s_r[:, :, 0], e_row[:, :], ALU.add))
                link(dve.memset(s_r[:, 0:EARLY + 1, 2], 1.0))
                link(dve.tensor_tensor(s_r[:, EARLY + 1:STEPS, 2], s_r[:, EARLY + 1:STEPS, 1],
                                       s_r[:, EARLY:STEPS - 1, 1], ALU.not_equal))
                dve.tensor_copy(sched[:, :, :], s_r[:, :, :]).then_inc(phase1, 1)

            neg_part(LAST, 0)
            neg_part(LAST, 1)
            elu(LAST, 0)
            elu(LAST, 1)
            norm(LAST, 0)
            norm(LAST, 1)
            for m in range(4):
                w1_rest(0, m)
                if m < 2:
                    xt_rest(LAST, m)
            xe_rest(0)
            experts(LAST)
            for m in range(4):
                w2_rest(0, m)
            slots(LAST)
            step(0, True, False, 0)
            schedule()
            step(1, True, True, 1)
            step(2, True, True, 2)
            with dve.Fori(3, STEPS - 1) as s:
                step(s, True, True, 2)
            step(STEPS - 1, False, False, 2)
            weigh(STEPS - 1, False)

        @block.tensor
        def _(pe):
            def three(dst, a_h, a_l, b_h, b_l, start, stop):
                pe.matmul(dst, a_h, b_h, start=start, stop=False)
                pe.matmul(dst, a_h, b_l, start=False, stop=False)
                return pe.matmul(dst, a_l, b_h, start=False, stop=stop)

            def transpose_n(j):
                pe.wait_ge(xn_done, j + 1)
                if j >= 2:
                    pe.wait_ge(nt_lo_done, j - 1)
                for d in range(DC):
                    last = pe.transpose(bank[BN + j % 2][:, d * P:(d + 1) * P], x_n[:, j % 2, d * P:(d + 1) * P],
                                        ident[:, :])
                last.then_inc(nt_ready, 1)

            def project(j):
                pe.wait_ge(nt_lo_done, j + 1)
                if j >= 2:
                    pe.wait_ge(zs_lo_done, j - 1)
                for d in range(DC):
                    if j == 0:
                        pe.wait_ge(w_lo_done, d + 1)
                    last = three(bank[BZ + j % 2][:, :], nt_hi[:, j % 2, d, :], nt_lo[:, j % 2, d, :],
                                 w_hi[:, d, :], w_lo[:, d, :], d == 0, d == DC - 1)
                last.then_inc(z_ready, 1)

            def transpose_x(p, q):
                t = 2 * p + q
                pe.wait_ge(xl_done, t + 1)
                if t == 0:
                    pe.wait_ge(nt_lo_done, NT)
                else:
                    pe.wait_ge(xt_lo_done, t)
                if p > 0:
                    pe.wait_ge(g_done, GC * p)
                for d in range(DC):
                    last = pe.transpose(bank[BG][:, d * P:(d + 1) * P], x_n[:, q, d * P:(d + 1) * P],
                                        ident[:, :])
                last.then_inc(xt_ready, 1)

            def gate(p):
                pe.wait_ge(xt_lo_done, 2 * p + 2)
                pe.wait_ge(gw1_lo_done, 1)
                for hb in range(GC):
                    for d in range(DC):
                        last = three(bank[BG][:, hb * 256:(hb + 1) * 256],
                                     gw1_hi[:, d, hb * P:(hb + 1) * P], gw1_lo[:, d, hb * P:(hb + 1) * P],
                                     xt_hi[:, d, :], xt_lo[:, d, :], d == 0, d == DC - 1)
                last.then_inc(g_ready, 1)

            def logits(p):
                pe.wait_ge(g_done, GC * (p + 1))
                pe.wait_ge(const_ld, 48)
                if p > 0:
                    pe.wait_ge(route_done, p)
                for q in range(2):
                    for hb in range(GC):
                        last = pe.matmul(bank[BS][:, L_AT + q * E:L_AT + (q + 1) * E], g_t[:, hb, q * P:(q + 1) * P],
                                         gw2_sb[:, hb, :], start=hb == 0, stop=hb == GC - 1)
                last.then_inc(l_ready, 1)

            def ranks(p):
                pe.wait_ge(mask_done, p + 1)
                r = bank[BS]
                pe.matmul(r[:, R_AT:R_AT + E], upper[:, :], mask[:, 0, :], start=True, stop=True)
                pe.matmul(r[:, R_AT + E:R_AT + 2 * E], upper[:, :], mask[:, 1, :], start=True, stop=False)
                pe.matmul(r[:, R_AT + E:R_AT + 2 * E], ones_bf[:, :], mask[:, 0, :], start=False, stop=True)
                pe.matmul(r[:, C_AT:C_AT + E], ones_bf[:, :], mask[:, 0, :], start=True, stop=False)
                pe.matmul(r[:, C_AT:C_AT + E], ones_bf[:, :], mask[:, 1, :], start=False,
                          stop=True).then_inc(r_ready, 1)

            post = events([("xt0", lambda p: transpose_x(p, 0)), ("xt1", lambda p: transpose_x(p, 1)),
                           ("gate", gate), ("logit", logits), ("rank", ranks)], 0)
            pe.wait_ge(consts, 1)

            def unit(u):
                j, c = units[u]
                if c == 0:
                    pe.wait_ge(zs_lo_done, j + 1)
                pe.wait_ge(a_lo_done, u + 1)
                k = u % RING
                for i in range(chunk_tiles(c)):
                    t = c * CT + i
                    if first(u):
                        if BZ <= t < N_SUM:
                            pe.wait_ge(zs_lo_done, NT)
                        elif t >= N_SUM:
                            pe.wait_ge(bank_read, t - N_SUM + 1)
                    last = three(bank[bank_no(t)][:, :], a_hi[:, k, i * P:(i + 1) * P], a_lo[:, k, i * P:(i + 1) * P],
                                 zs_hi[:, j, :], zs_lo[:, j, :], first(u), closes(u))
                    if closes(u):
                        last.then_inc(bank_full, 1)
                if not closes(u):
                    last.then_inc(unit_done, 1)

            transpose_n(0)
            transpose_n(1)
            project(0)
            for j in range(NT):
                if j + 2 < NT:
                    transpose_n(j + 2)
                if j + 1 < NT:
                    project(j + 1)
                unit(j)
            for u in range(NT, NU):
                run(post, u - 1)
                unit(u)
            run(post, NU - 1)
            finish(post)

            def transpose_xe(s, first):
                if first:
                    pe.wait_ge(bank_read, NT)
                else:
                    pe.wait_ge(xe_lo_done, SJ * s)
                for jj in range(SJ):
                    pe.wait_ge(xg_ld, 16 * (SJ * s + SJ))
                    for d in range(DC):
                        last = pe.transpose(bank[jj][:, d * P:(d + 1) * P], x_g[:, jj, d * P:(d + 1) * P],
                                            ident[:, :])
                    last.then_inc(xe_ready, 1)

            def step(s, nxt, first):
                pe.wait_ge(xe_lo_done, SJ * s + SJ)
                for k in range(HC):
                    if first and k == HC // 2:
                        ranks(LAST)
                    if k % 2 == 0:
                        pe.wait_ge(w1_lo_done, 4 * weights(s) + k // 2 + 1)
                        if not first:
                            pe.wait_ge(h_lo_done, 4 * (s - 1) + k // 2 + 1)
                    for d in range(DC):
                        last = three(bank[2 + k // 2][:, k % 2 * 256:k % 2 * 256 + 256],
                                     w1_hi[:, d, k * P:(k + 1) * P], w1_lo[:, d, k * P:(k + 1) * P],
                                     xe_hi[:, d, :], xe_lo[:, d, :], d == 0, d == DC - 1)
                    last.then_inc(h_ready, 1)
                if nxt:
                    transpose_xe(s + 1, False)
                if first:
                    pe.wait_ge(route_done, N_PAIR)
                else:
                    pe.wait_ge(yw_done, SJ * s)
                for k in range(HC):
                    if k % 2 == 0:
                        pe.wait_ge(w2_lo_done, 4 * weights(s) + k // 2 + 1)
                        pe.wait_ge(h_lo_done, 4 * s + k // 2 + 1)
                    for jj in range(SJ):
                        last = three(bank[6 + jj][:, :], h_hi[:, k, jj * P:(jj + 1) * P], h_lo[:, k, jj * P:(jj + 1) * P],
                                     w2_hi[:, k, :], w2_lo[:, k, :], k == 0, k == HC - 1)
                        if k == HC - 1:
                            last.then_inc(ye_ready, 1)
                        elif k % 2 and jj == SJ - 1:
                            last.then_inc(w2_used, 1)

            transpose_x(LAST, 0)
            transpose_x(LAST, 1)
            gate(LAST)
            transpose_xe(0, True)
            logits(LAST)
            step(0, True, True)
            for s in range(1, EARLY + 1):
                step(s, True, False)
            with pe.Fori(EARLY + 1, STEPS - 1) as s:
                step(s, True, False)
            step(STEPS - 1, False, False)


def kernel(x, adj, L0_gnn_w, L0_ffn_gw1, L0_ffn_gb1, L0_ffn_gw2, L0_ffn_gb2, L0_ffn_we1, L0_ffn_be1,
           L0_ffn_we2, L0_ffn_be2):
    import numpy as np
    import concourse.bacc as bacc
    from concourse import mybir as mb
    from concourse.bass_utils import run_bass_kernel_spmd

    x_p = np.zeros((NP, D), np.float32)
    x_p[:N_TOK] = np.asarray(x)
    a_p = np.zeros((NP, NP), np.float32)
    a_p[:N_TOK, :N_TOK] = np.asarray(adj)
    arrays = {
        "x_in": x_p,
        "adj_in": a_p,
        "adj_t_in": np.ascontiguousarray(a_p.T),
        "w_in": np.ascontiguousarray(L0_gnn_w),
        "gw1_in": np.ascontiguousarray(L0_ffn_gw1),
        "gb1_in": np.ascontiguousarray(np.asarray(L0_ffn_gb1).reshape(GC, P).T),
        "gw2_in": np.ascontiguousarray(L0_ffn_gw2),
        "gb2_in": np.ascontiguousarray(L0_ffn_gb2),
        "we1_in": np.ascontiguousarray(L0_ffn_we1),
        "be1_in": np.ascontiguousarray(np.asarray(L0_ffn_be1).reshape(E, HC, P).transpose(0, 2, 1)),
        "we2_in": np.ascontiguousarray(L0_ffn_we2),
        "be2_in": np.ascontiguousarray(L0_ffn_be2),
    }
    nc = bacc.Bacc("TRN2", target_bir_lowering=False, num_devices=1)
    args = [nc.dram_tensor(n, a.shape, mb.dt.from_np(a.dtype), kind="ExternalInput").ap() for n, a in arrays.items()]
    args.append(nc.dram_tensor("out_rows", (ROWS, D), F32, kind="ExternalOutput").ap())
    build(nc, *args)
    r = run_bass_kernel_spmd(nc, [arrays], core_ids=[0])
    return r.results[0]["out_rows"][:N_TOK]
```
